# Optimizing a Trainium2 kernel written in Bass

```python
import numpy as np
import jax
import jax.numpy as jnp

def _softmax(x, axis=-1):
    return jax.nn.softmax(x, axis=axis)

def _gelu(x):
    return jax.nn.gelu(x, approximate=True)

def _silu(x):
    return jax.nn.silu(x)

def _sigmoid(x):
    return jax.nn.sigmoid(x)

def _layernorm(x, axis=-1, eps=1e-05):
    m = jnp.mean(x, axis=axis, keepdims=True)
    v = jnp.var(x, axis=axis, keepdims=True)
    return (x - m) / jnp.sqrt(v + eps)

def _scatter_add(tgt, idx, src, axis=0):
    return tgt.at[idx].add(src)

def _segment_sum(src, seg, n):
    return jax.ops.segment_sum(src, seg, n)
kernel_name = 'mk_flamingo_gated_d2_seqx_r4_d5ae61'

def setup_inputs(seed: int=0):
    np.random.seed(seed)
    _w = jnp.asarray

    def _rec_inputs():
        import jax
        import jax.numpy as jnp
        _rk = jax.random.key(seed)
        x = 7.22e-05 + 1 * jax.random.normal(jax.random.fold_in(_rk, 1), (32, 128, 256), jnp.float32)
        _lenS = 128 - jax.random.randint(jax.random.fold_in(_rk, 7), (32,), 0, max(1, 128 // 4) + 1, jnp.int32)
        _lenS2 = 128 - jax.random.randint(jax.random.fold_in(_rk, 8), (32,), 0, max(1, 128 // 4) + 1, jnp.int32)
        _ctx_1024P = jax.random.normal(jax.random.fold_in(_rk, 11), (32, 16, 256), jnp.float32)
        _ctx_1024c = jax.random.dirichlet(jax.random.fold_in(_rk, 511), 0.3 * jnp.ones((16,), jnp.float32), (32, 128))
        _ctx_1024t = jnp.einsum('bsk,bkd->bsd', _ctx_1024c, _ctx_1024P)
        _ctx_1024t = _ctx_1024t * jax.lax.rsqrt(jnp.mean(jnp.square(_ctx_1024t)) + 1e-12) * 0.953939
        ctx_1024 = 4.13588e-05 + 0.999923 * (_ctx_1024t + 0.3 * jax.random.normal(jax.random.fold_in(_rk, 611), (32, 128, 256), jnp.float32))
        _g = jax.random.normal(jax.random.fold_in(_rk, 9001), (2, 2), jnp.float32)
        _g = jnp.sign(_g) * jnp.maximum(jnp.abs(_g), 1.0) + (_g == 0) * 1.0
        g_xattn = _g[0]
        g_ffn = _g[1]
        return (x, ctx_1024, g_xattn, g_ffn)
    x, ctx_1024, g_xattn, g_ffn = _rec_inputs()

    def _L0_xattn_setup():
        import jax, jax.numpy as jnp
        import numpy as np
        THETA = 10000.0
        SCALE_BASE = 512.0
        GAMMA = 0.96875

        def _dup_interleave(x):
            return jnp.repeat(x, 2, axis=-1)

        def _xpos(x, offset, inverse_scale):
            L, d = (x.shape[-2], x.shape[-1])
            half = d // 2
            base = (jnp.arange(0, d, 2, dtype=x.dtype) + 0.4 * d) / (1.4 * d)
            pos = jnp.arange(offset, offset + L, dtype=x.dtype)
            scale = base[None, :] ** (pos[:, None] / SCALE_BASE)
            freqs = 1.0 / THETA ** (jnp.arange(half, dtype=x.dtype) / half)
            sin_in = pos[:, None] * freqs[None, :]
            if inverse_scale:
                scale = 1.0 / scale
            sin = _dup_interleave(jnp.sin(sin_in) * scale)
            cos = _dup_interleave(jnp.cos(sin_in) * scale)
            rot = jnp.stack((-x[..., 1::2], x[..., ::2]), axis=-1).reshape(x.shape)
            return x * cos + rot * sin

        def _decay_mask(L, gamma, dtype):
            u = jnp.arange(L, dtype=dtype)[:, None]
            v = jnp.arange(L, dtype=dtype)[None, :]
            return jnp.where(u >= v, gamma ** (u - v), jnp.zeros((), dtype))
        key = jax.random.key(seed)
        ks = jax.random.split(key, 6)
        B, L, E = (2, 1024, 256)
        query = jax.random.normal(ks[0], (B, L, E), jnp.float32)
        k_in = jax.random.normal(ks[1], (B, L, E), jnp.float32)
        value = jax.random.normal(ks[2], (B, L, E), jnp.float32)
        s = 1.0 / np.sqrt(E)
        Wq = jax.random.normal(ks[3], (E, E), jnp.float32) * s
        Wk = jax.random.normal(ks[4], (E, E), jnp.float32) * s
        Wv = jax.random.normal(ks[5], (E, E), jnp.float32) * s
        return {'query': query, 'key': k_in, 'value': value, 'Wq': Wq, 'Wk': Wk, 'Wv': Wv}
    _L0_xattn_all = _L0_xattn_setup()
    _L0_xattn_in = {k: v for k, v in _L0_xattn_all.items() if k in ('Wq', 'Wk', 'Wv')}
    del _L0_xattn_all

    def _L0_ffn_setup():
        import jax, jax.numpy as jnp
        import numpy as np
        IN_DIM = 256
        OUT_DIM = 256
        NUM_EXPERTS = 8
        TOP_K = 2
        key = jax.random.key(seed)
        ks = jax.random.split(key, 5)
        s = 1.0 / np.sqrt(IN_DIM)
        x = jax.random.normal(ks[0], (4, 512, IN_DIM), dtype=jnp.float32)
        Wg = jax.random.uniform(ks[1], (IN_DIM, NUM_EXPERTS), jnp.float32, -s, s)
        bg = jnp.zeros((NUM_EXPERTS,), jnp.float32)
        We = jax.random.uniform(ks[2], (NUM_EXPERTS, OUT_DIM, IN_DIM), jnp.float32, -s, s)
        be = jax.random.uniform(ks[3], (NUM_EXPERTS, OUT_DIM), jnp.float32, -s, s)
        return {'x': x, 'Wg': Wg, 'bg': bg, 'We': We, 'be': be}
    _L0_ffn_all = _L0_ffn_setup()
    _L0_ffn_in = {k: v for k, v in _L0_ffn_all.items() if k in ('Wg', 'bg', 'We', 'be')}
    del _L0_ffn_all

    def _L1_xattn_setup():
        import jax, jax.numpy as jnp
        import numpy as np
        D_MODEL = 256
        N_HEAD = 16
        HEAD_DIM = D_MODEL // N_HEAD
        key = jax.random.key(seed)
        ks = jax.random.split(key, 9)
        B, T = (2, 512)
        s = 0.02
        return {'k': jax.random.normal(ks[0], (B, T, D_MODEL), jnp.float32), 'q': jax.random.normal(ks[1], (B, T, D_MODEL), jnp.float32), 'v': jax.random.normal(ks[2], (B, T, D_MODEL), jnp.float32), 'Wk': jax.random.normal(ks[3], (D_MODEL, D_MODEL), jnp.float32) * s, 'bk': jnp.zeros((D_MODEL,), jnp.float32), 'Wq': jax.random.normal(ks[4], (D_MODEL, D_MODEL), jnp.float32) * s, 'bq': jnp.zeros((D_MODEL,), jnp.float32), 'Wc': jax.random.normal(ks[5], (D_MODEL, D_MODEL), jnp.float32) * s, 'bc': jnp.zeros((D_MODEL,), jnp.float32)}
    _L1_xattn_all = _L1_xattn_setup()
    _L1_xattn_in = {k: v for k, v in _L1_xattn_all.items() if k in ('Wk', 'bk', 'Wq', 'bq', 'Wc', 'bc')}
    del _L1_xattn_all

    def _L1_ffn_setup():
        import jax, jax.numpy as jnp
        import numpy as np
        N_HEADS = 16
        NUM_EXPERTS = 4
        TOP_K = 2
        D_MODEL = 256
        GATE_HID = 128
        key = jax.random.key(seed)
        ks = jax.random.split(key, 12)
        B, T, C, E = (2, 256, D_MODEL, NUM_EXPERTS)
        s = 1.0 / np.sqrt(C)
        return {'hidden_states': jax.random.normal(ks[0], (B, T, C), jnp.float32), 'Wq': jax.random.normal(ks[1], (E, C, C), jnp.float32) * s, 'bq': jnp.zeros((E, C), jnp.float32), 'Wk': jax.random.normal(ks[2], (E, C, C), jnp.float32) * s, 'bk': jnp.zeros((E, C), jnp.float32), 'Wv': jax.random.normal(ks[3], (E, C, C), jnp.float32) * s, 'bv': jnp.zeros((E, C), jnp.float32), 'Wg1': jax.random.normal(ks[4], (C, GATE_HID), jnp.float32) * s, 'bg1': jnp.zeros((GATE_HID,), jnp.float32), 'Wg2': jax.random.normal(ks[5], (GATE_HID, E), jnp.float32) / np.sqrt(GATE_HID), 'bg2': jnp.zeros((E,), jnp.float32), 'Wo': jax.random.normal(ks[6], (C, C), jnp.float32) * s, 'bo': jnp.zeros((C,), jnp.float32)}
    _L1_ffn_all = _L1_ffn_setup()
    _L1_ffn_in = {k: v for k, v in _L1_ffn_all.items() if k in ('Wq', 'bq', 'Wk', 'bk', 'Wv', 'bv', 'Wg1', 'bg1', 'Wg2', 'bg2', 'Wo', 'bo')}
    del _L1_ffn_all
    return {'x': x, 'ctx_1024': ctx_1024, 'g_xattn': g_xattn, 'g_ffn': g_ffn, 'L0_xattn_Wq': _L0_xattn_in['Wq'], 'L0_xattn_Wk': _L0_xattn_in['Wk'], 'L0_xattn_Wv': _L0_xattn_in['Wv'], 'L0_ffn_Wg': _L0_ffn_in['Wg'], 'L0_ffn_bg': _L0_ffn_in['bg'], 'L0_ffn_We': _L0_ffn_in['We'], 'L0_ffn_be': _L0_ffn_in['be'], 'L1_xattn_Wk': _L1_xattn_in['Wk'], 'L1_xattn_bk': _L1_xattn_in['bk'], 'L1_xattn_Wq': _L1_xattn_in['Wq'], 'L1_xattn_bq': _L1_xattn_in['bq'], 'L1_xattn_Wc': _L1_xattn_in['Wc'], 'L1_xattn_bc': _L1_xattn_in['bc'], 'L1_ffn_Wq': _L1_ffn_in['Wq'], 'L1_ffn_bq': _L1_ffn_in['bq'], 'L1_ffn_Wk': _L1_ffn_in['Wk'], 'L1_ffn_bk': _L1_ffn_in['bk'], 'L1_ffn_Wv': _L1_ffn_in['Wv'], 'L1_ffn_bv': _L1_ffn_in['bv'], 'L1_ffn_Wg1': _L1_ffn_in['Wg1'], 'L1_ffn_bg1': _L1_ffn_in['bg1'], 'L1_ffn_Wg2': _L1_ffn_in['Wg2'], 'L1_ffn_bg2': _L1_ffn_in['bg2'], 'L1_ffn_Wo': _L1_ffn_in['Wo'], 'L1_ffn_bo': _L1_ffn_in['bo']}

def reference(x, ctx_1024, g_xattn, g_ffn, L0_xattn_Wq, L0_xattn_Wk, L0_xattn_Wv, L0_ffn_Wg, L0_ffn_bg, L0_ffn_We, L0_ffn_be, L1_xattn_Wk, L1_xattn_bk, L1_xattn_Wq, L1_xattn_bq, L1_xattn_Wc, L1_xattn_bc, L1_ffn_Wq, L1_ffn_bq, L1_ffn_Wk, L1_ffn_bk, L1_ffn_Wv, L1_ffn_bv, L1_ffn_Wg1, L1_ffn_bg1, L1_ffn_Wg2, L1_ffn_bg2, L1_ffn_Wo, L1_ffn_bo):
    import jax
    import jax.numpy as jnp

    def _L0_xattn_ref(query, key, value, Wq, Wk, Wv):
        import jax, jax.numpy as jnp
        import numpy as np
        THETA = 10000.0
        SCALE_BASE = 512.0
        GAMMA = 0.96875

        def _dup_interleave(x):
            return jnp.repeat(x, 2, axis=-1)

        def _xpos(x, offset, inverse_scale):
            L, d = (x.shape[-2], x.shape[-1])
            half = d // 2
            base = (jnp.arange(0, d, 2, dtype=x.dtype) + 0.4 * d) / (1.4 * d)
            pos = jnp.arange(offset, offset + L, dtype=x.dtype)
            scale = base[None, :] ** (pos[:, None] / SCALE_BASE)
            freqs = 1.0 / THETA ** (jnp.arange(half, dtype=x.dtype) / half)
            sin_in = pos[:, None] * freqs[None, :]
            if inverse_scale:
                scale = 1.0 / scale
            sin = _dup_interleave(jnp.sin(sin_in) * scale)
            cos = _dup_interleave(jnp.cos(sin_in) * scale)
            rot = jnp.stack((-x[..., 1::2], x[..., ::2]), axis=-1).reshape(x.shape)
            return x * cos + rot * sin

        def _decay_mask(L, gamma, dtype):
            u = jnp.arange(L, dtype=dtype)[:, None]
            v = jnp.arange(L, dtype=dtype)[None, :]
            return jnp.where(u >= v, gamma ** (u - v), jnp.zeros((), dtype))
        q = jnp.einsum('ble,de->bld', query, Wq)
        k = jnp.einsum('ble,de->bld', key, Wk)
        v = jnp.einsum('ble,de->bld', value, Wv)
        q = _xpos(q, 0, False)
        k = _xpos(k, 0, True)
        L = q.shape[-2]
        mask = _decay_mask(L, jnp.asarray(GAMMA, q.dtype), q.dtype)
        retention = jnp.einsum('bqd,bkd->bqk', q, k) * mask[None, :, :]
        out = jnp.einsum('bqk,bkv->bqv', retention, v)
        return out

    def _L0_ffn_ref(x, Wg, bg, We, be):
        import jax, jax.numpy as jnp
        import numpy as np
        IN_DIM = 256
        OUT_DIM = 256
        NUM_EXPERTS = 8
        TOP_K = 2
        gate = jax.nn.softmax(x @ Wg + bg, axis=-1)
        topk_vals, topk_idx = jax.lax.top_k(gate, TOP_K)
        onehot = jax.nn.one_hot(topk_idx, NUM_EXPERTS, dtype=gate.dtype)
        gate_sparse = jnp.einsum('bsk,bske->bse', topk_vals, onehot)
        gate_sparse = gate_sparse / jnp.sum(gate_sparse, axis=-1, keepdims=True)
        y = jnp.einsum('bsi,eoi->bseo', x, We) + be[None, None, :, :].transpose(0, 1, 2, 3)
        out = jnp.einsum('bseo,bse->bso', y, gate_sparse)
        return out

    def _L1_xattn_ref(k, q, v, Wk, bk, Wq, bq, Wc, bc):
        import jax, jax.numpy as jnp
        import numpy as np
        D_MODEL = 256
        N_HEAD = 16
        HEAD_DIM = D_MODEL // N_HEAD
        B, T_v, C = v.shape
        T_q = q.shape[1]
        H, hd = (N_HEAD, C // N_HEAD)
        kp = k @ Wk.T + bk
        qp = q @ Wq.T + bq
        kh = kp.reshape(B, T_v, H, hd).transpose(0, 2, 1, 3)
        qh = qp.reshape(B, T_q, H, hd).transpose(0, 2, 1, 3)
        vh = v.reshape(B, T_v, H, hd).transpose(0, 2, 1, 3)
        scale = 1.0 / jnp.sqrt(jnp.asarray(hd, kh.dtype))
        att = jnp.einsum('bhqd,bhkd->bhqk', qh, kh) * scale
        att = jax.nn.softmax(att, axis=-1)
        y = jnp.einsum('bhqk,bhkd->bhqd', att, vh)
        y = y.transpose(0, 2, 1, 3).reshape(B, T_q, C)
        return y @ Wc.T + bc

    def _L1_ffn_ref(hidden_states, Wq, bq, Wk, bk, Wv, bv, Wg1, bg1, Wg2, bg2, Wo, bo):
        import jax, jax.numpy as jnp
        import numpy as np
        N_HEADS = 16
        NUM_EXPERTS = 4
        TOP_K = 2
        D_MODEL = 256
        GATE_HID = 128
        B, T, C = hidden_states.shape
        H = N_HEADS
        D = C // H
        pooled = hidden_states.mean(axis=1)
        logits = jax.nn.relu(pooled @ Wg1 + bg1) @ Wg2 + bg2
        vals, idx = jax.lax.top_k(logits, TOP_K)
        sm = jax.nn.softmax(vals, axis=-1)
        weights = jnp.zeros_like(logits).at[jnp.arange(B)[:, None], idx].set(sm)

        def moe_proj(W, b):
            Wc = jnp.einsum('be,ecd->bcd', weights, W)
            bc = weights @ b
            return jnp.einsum('btc,bcd->btd', hidden_states, Wc) + bc[:, None, :]
        q = moe_proj(Wq, bq).reshape(B, T, H, D)
        k = moe_proj(Wk, bk).reshape(B, T, H, D)
        v = moe_proj(Wv, bv).reshape(B, T, H, D)
        scores = jnp.einsum('bthd,bshd->bhts', q, k) / np.sqrt(D).astype(np.float32)
        attn = jax.nn.softmax(scores, axis=-1)
        out = jnp.einsum('bhts,bshd->bthd', attn, v).reshape(B, T, C)
        return out @ Wo + bo
    x = x + jnp.tanh(g_xattn[0]) * _L0_xattn_ref(_layernorm(x, axis=-1), ctx_1024, ctx_1024, L0_xattn_Wq, L0_xattn_Wk, L0_xattn_Wv)
    x = x + jnp.tanh(g_ffn[0]) * _L0_ffn_ref(_layernorm(x, axis=-1), L0_ffn_Wg, L0_ffn_bg, L0_ffn_We, L0_ffn_be)
    x = x + jnp.tanh(g_xattn[1]) * _L1_xattn_ref(ctx_1024, _layernorm(x, axis=-1), ctx_1024, L1_xattn_Wk, L1_xattn_bk, L1_xattn_Wq, L1_xattn_bq, L1_xattn_Wc, L1_xattn_bc)
    x = x + jnp.tanh(g_ffn[1]) * _L1_ffn_ref(_layernorm(x, axis=-1), L1_ffn_Wq, L1_ffn_bq, L1_ffn_Wk, L1_ffn_bk, L1_ffn_Wv, L1_ffn_bv, L1_ffn_Wg1, L1_ffn_bg1, L1_ffn_Wg2, L1_ffn_bg2, L1_ffn_Wo, L1_ffn_bo)
    return x

_drawn_inputs = setup_inputs


def setup_inputs(seed=0):
    import zlib

    import numpy as np

    out = dict(_drawn_inputs(seed))
    spreads = {'g_ffn': (-1.0, 0.6),
     'L0_ffn_bg': (0.0, 0.8),
     'L1_xattn_bk': (0.0, 0.8),
     'L1_xattn_bq': (0.0, 0.8),
     'L1_xattn_bc': (0.0, 0.8),
     'L1_ffn_bq': (0.0, 0.8),
     'L1_ffn_bk': (0.0, 0.8),
     'L1_ffn_bv': (0.0, 0.8),
     'L1_ffn_bg1': (0.0, 0.8),
     'L1_ffn_bg2': (0.0, 0.8),
     'L1_ffn_bo': (0.0, 0.8)}
    factors = {'L0_ffn_Wg': 8.0,
     'L0_ffn_We': 8.0,
     'L0_ffn_be': 8.0,
     'L1_xattn_Wk': 8.0,
     'L1_xattn_Wq': 8.0,
     'L1_xattn_Wc': 8.0,
     'L1_ffn_Wq': 8.0,
     'L1_ffn_Wk': 8.0,
     'L1_ffn_Wv': 8.0,
     'L1_ffn_Wg1': 8.0,
     'L1_ffn_Wg2': 8.0,
     'L1_ffn_Wo': 8.0}
    for name, (base, spread) in spreads.items():
        noise = np.random.default_rng([zlib.crc32(name.encode()), seed]).standard_normal(out[name].shape)
        drawn = base * np.exp(spread * noise) if base else spread * noise
        out[name] = jnp.asarray(drawn.astype(out[name].dtype))
    for name, factor in factors.items():
        out[name] = (out[name] * factor).astype(out[name].dtype)
    return out
```

```python
import numpy as np
import concourse.bass as bass
from concourse import mybir
from contextlib import ExitStack

F32 = mybir.dt.float32
U32 = mybir.dt.uint32
ALU = mybir.AluOpType
ACT = mybir.ActivationFunctionType
AX = mybir.AxisListType

NB = 32
P = 128
D = 256
KT = D // P
H = 16
HD = D // H
NG = 4
GH = H // NG
E0 = 8
E1 = 4
GAMMA = 0.96875
EPS = 1e-5
SCALE = 1.0 / float(np.sqrt(HD))
NEG = -3.0e38

LAG = {"a": 0, "b": 1, "c": 2, "d": 3, "e": 4}
DEPTH = max(LAG.values())

ORDER = [
    "b_ln", "d_ln", "c_ln", "e_s0", "b_tr", "e_s1", "d_tr", "e_t0", "c_tr", "e_s2", "b_g", "e_t1", "e_v0",
    "e_s3", "d_h", "e_t2", "e_v1", "c_qk", "a_ln", "e_t3", "e_v2", "b_w", "d_lg", "e_v3",
    "a_tr", "e_z0", "b_be", "d_w", "e_z1", "c_s0", "b_m0", "d_c0", "a_qk", "c_s1", "e_yt", "c_t0", "b_m1", "d_c1",
    "c_s2", "a_v", "c_t1", "c_v0", "e_o", "c_s3", "a_tr2", "b_m2", "d_c2", "c_t2", "c_v1", "a_r", "c_t3", "c_v2",
    "d_qk", "b_m3", "c_v3", "c_z0", "d_v", "a_o", "c_z1", "c_yt", "c_o",
]
BANK = {
    "a_tr": "M0", "a_qk": "M0", "a_v": "M0", "a_tr2": "M0", "a_r": "M0", "a_o": "M0",
    "b_tr": "M1", "b_g": "M1", "b_w": "M1", "b_be": "M1", "b_m0": "M1", "b_m1": "M1", "b_m2": "M1", "b_m3": "M1",
    "c_tr": "TC", "c_qk": "SC", "c_z1": "SC", "c_yt": "TC", "c_o": "ZC", "c_v": "ZC",
    "d_tr": "M0", "d_h": "M0", "d_lg": "M0", "d_qk": "SE", "d_v": "TE",
    "e_z1": "SE", "e_yt": "TE", "e_o": "ZE", "e_v": "ZE",
}
for _g in range(NG):
    BANK[f"c_s{_g}"], BANK[f"e_s{_g}"] = "SC", "SE"
    BANK[f"c_t{_g}"], BANK[f"e_t{_g}"] = "TC", "TE"
TAKES = {s: (BANK["c_v"] if s[0] == "c" else BANK["e_v"]) if s[2:] == "v0" else BANK.get(s) for s in ORDER}


GROUPED = {s for s in ORDER if s[0] in "ce" and s[2] in "stv" and s[3].isdigit()}


def before(bank, step, t):
    users = [s for s in ORDER if TAKES[s] == bank]
    at = users.index(step)
    for back in range(1, len(users) * (DEPTH + 2) + 1):
        user, turns = users[(at - back) % len(users)], (at - back) // len(users)
        batch = t - LAG[user[0]] + turns
        if not isinstance(t, int) or 0 <= batch < NB:
            return user, batch
    return None


WEIGHTS = [
    ("wq0", KT * D), ("wk0", KT * D), ("wv0", KT * D), ("we", KT * E0 * D), ("be", D), ("wgate", KT * P), ("bgate", E0),
    ("wq1", KT * D), ("wk1", KT * D), ("bq1", KT), ("bk1", KT), ("wc1", KT * D), ("bc1", D),
    ("wx", E1 * 3 * KT * D), ("bx", E1 * 3 * KT), ("wh", KT * P), ("bh", 1), ("wl", E0), ("bl", E0),
    ("wo", KT * D), ("bo", D), ("g", 4),
]
TABLES = [
    ("cos", 2 * D), ("sin", 2 * D), ("decay", P), ("ident", P), ("heads", E0), ("iota", E0), ("eps", 2),
]


def build(nc, x, ctx_in, weights, tables, out):
    with ExitStack() as stack:
        def sb(name, *shape, dt=F32):
            return stack.enter_context(nc.sbuf_tensor(name, [P, *shape], dt))

        wsum, tsum = sum(n for _, n in WEIGHTS), sum(n for _, n in TABLES)
        w_sb, t_sb = sb("w_sb", wsum), sb("t_sb", tsum)
        c = {}
        for tile, parts in ((w_sb, WEIGHTS), (t_sb, TABLES)):
            at = 0
            for name, n in parts:
                c[name] = tile[:, at:at + n]
                at += n
        wq0 = c["wq0"].rearrange("p (k n) -> p k n", k=KT)
        wk0 = c["wk0"].rearrange("p (k n) -> p k n", k=KT)
        wv0 = c["wv0"].rearrange("p (k n) -> p k n", k=KT)
        we = c["we"].rearrange("p (k n) -> p k n", k=KT)
        wgate = c["wgate"].rearrange("p (k n) -> p k n", k=KT)
        wq1 = c["wq1"].rearrange("p (k n) -> p k n", k=KT)
        wk1 = c["wk1"].rearrange("p (k n) -> p k n", k=KT)
        wc1 = c["wc1"].rearrange("p (k n) -> p k n", k=KT)
        wx = c["wx"].rearrange("p (e n) -> p e n", e=E1)
        bx = c["bx"].rearrange("p (e n) -> p e n", e=E1)
        wh = c["wh"].rearrange("p (k n) -> p k n", k=KT)
        wo = c["wo"].rearrange("p (k n) -> p k n", k=KT)
        ident = c["ident"]

        tg = sb("tg", 4)
        gbc, gbo = sb("gbc", D), sb("gbo", D)
        bq1s = sb("bq1s", KT)
        ones, carrier = sb("ones", P), sb("carrier", 1)

        a_x, a_ctx, a_xn = sb("a_x", D), sb("a_ctx", D), sb("a_xn", D)
        a_t, a_qk, a_qkt = sb("a_t", 2 * KT, P), sb("a_qk", 2 * D), sb("a_qkt", 2 * KT, P)
        a_c, a_s = sb("a_c", 2 * D), sb("a_s", 2 * D)
        a_v, a_ret = sb("a_v", D), sb("a_ret", P)
        b_x, b_xn, b_t = sb("b_x", D), sb("b_xn", D), sb("b_t", KT, P)
        b_wt, b_wtt, b_acc = sb("b_wt", P), sb("b_wtt", P), sb("b_acc", D)
        c_x, c_xb, c_xn, c_ctx, c_t = sb("c_x", D), sb("c_xb", D), sb("c_xn", D), sb("c_ctx", D), sb("c_t", 2 * KT, P)
        d_x, d_xn, d_t, d_pool = sb("d_x", D), sb("d_xn", D), sb("d_t", KT, P), sb("d_pool", KT)
        d_h, d_hb = sb("d_h", 1), sb("d_hb", P)
        d_wx, d_bx = sb("d_wx", 3, KT * D), sb("d_bx", 3 * KT)
        e_xb, e_out, e_bv = sb("e_xb", D), sb("e_out", D), sb("e_bv", KT)
        stats = {s: sb(f"{s}_stats", 6) for s in "abcd"}
        mv = {s: sb(f"{s}_mv", 2) for s in "abcd"}
        rstd = {s: sb(f"{s}_rstd", 2) for s in "abcd"}
        top = {s: {"lg": sb(f"{s}_lg", 8), "mx": sb(f"{s}_mx", 8), "ix": sb(f"{s}_ix", 8, dt=U32), "if": sb(f"{s}_if", 2),
                   "n": sb(f"{s}_n", 1), "e": sb(f"{s}_e", 1), "s": sb(f"{s}_s", 1), "r": sb(f"{s}_r", 2),
                   "w1": sb(f"{s}_w1", 8), "w2": sb(f"{s}_w2", 8), "w": sb(f"{s}_wts", 8)} for s in "bd"}
        qt = {s: sb(f"{s}_qt", KT, P) for s in "ce"}
        kt = {s: sb(f"{s}_kt", KT, P) for s in "ce"}
        kb = {s: sb(f"{s}_kb", KT, E0, P) for s in "ce"}
        v1 = {s: sb(f"{s}_v1", H, 2 * HD) for s in "ce"}
        mx = {s: sb(f"{s}_smx", H) for s in "ce"}
        sc = {s: sb(f"{s}_sc", 2, GH, P) for s in "ce"}
        pt = {s: sb(f"{s}_pt", 2, GH, P) for s in "ce"}
        z = {s: sb(f"{s}_z", NG, P) for s in "ce"}
        rz = {s: sb(f"{s}_rz", H) for s in "ce"}
        y = {s: sb(f"{s}_y", D) for s in "ce"}
        yt = {s: sb(f"{s}_yt", KT, P) for s in "ce"}

        bank = {n: stack.enter_context(nc.psum_tensor(n, [P, 512], F32)) for n in ("M0", "M1", "SC", "TC", "ZC", "SE", "TE", "ZE")}

        def psum(step):
            return bank[BANK[step[:3] if step[2] == "v" and step[0] in "ce" else step]][:, :]

        class Semaphores(dict):

            def __missing__(self, event):
                self[event] = stack.enter_context(nc.semaphore(event.replace(".", "_")))
                return self[event]

        sem = Semaphores()

        block = stack.enter_context(nc.Block())

        class Turn:

            def __init__(self, eng, t):
                self.eng, self.t, self.counts = eng, t, {}

            def count(self, per, n):
                if isinstance(self.t, int):
                    return max(self.t * per + n, 0)
                if (per, n) not in self.counts:
                    self.counts[per, n] = self.eng.snap(self.t * per + n)
                return self.counts[per, n]

            def done(self, stage):
                return self.count(1, 1 - LAG[stage])

            def last(self, stage):
                return self.count(1, -LAG[stage])

            def group_done(self, stage, g):
                return self.count(NG, -NG * LAG[stage] + g + 1)

            def group_last(self, stage, g):
                return self.count(NG, -NG * LAG[stage] + g + 1 - NG)

            def arrived(self, stage, each):
                return self.count(each, (1 - LAG[stage]) * each)

            def user(self, step):
                if isinstance(self.t, int):
                    return before(TAKES[step], step, self.t) or (step, -1)
                users = [s for s in ORDER if TAKES[s] == TAKES[step]]
                at = users.index(step)
                return users[at - 1], -LAG[users[at - 1][0]] - (at == 0)

            def reader(self, step):
                user, _ = self.user(step)
                if user[2:] == "v0":
                    return user[0] + "_z0.free"
                return user[:3] + ".free" if user in GROUPED else user + ".free"

            def released(self, step):
                user, batch = self.user(step)
                per, n = (NG, int(user[3]) + 1) if user in GROUPED and user[2] != "v" else (1, 1)
                if isinstance(self.t, int):
                    return max(batch * per + n, 0)
                return self.count(per, batch * per + n)

        def run(eng, step_fn):
            def turn(t, steps):
                now = Turn(eng, t)
                for s in steps:
                    step_fn(now, s)
            for t in range(DEPTH + 1):
                turn(t, [s for s in ORDER if t >= LAG[s[0]]])
            with eng.Fori(DEPTH + 1, NB) as t:
                turn(t, ORDER)
            for t in range(NB, NB + DEPTH):
                turn(t, [s for s in ORDER if t - LAG[s[0]] < NB])

        x_rows = x.rearrange("b p d -> (b p) d")
        ctx_rows = ctx_in.rearrange("b p d -> (b p) d")
        out_rows = out.rearrange("b p d -> (b p) d")

        @block.sync
        def _(sp):
            sp.dma_start(t_sb[:, :], tables).then_inc(sem["loaded"], 16)
            sp.dma_start(w_sb[:, :], weights).then_inc(sem["loaded"], 16)

            def rows(b):
                return bass.ds(b * P, P)

            def step(now, s):
                if s == "a_ln":
                    sp.wait_ge(sem["a_o.free"], now.last("a"))
                    sp.wait_ge(sem["a_tr.full"], now.last("a"))
                    sp.dma_start(a_x[:, :], x_rows[rows(now.t), :]).then_inc(sem["a_loaded"], 16)
                    sp.dma_start(a_ctx[:, :], ctx_rows[rows(now.t), :]).then_inc(sem["a_loaded"], 16)
                if s == "c_ln":
                    sp.wait_ge(sem["c_tr.full"], now.last("c"))
                    sp.wait_ge(sem["c_v1_done"], now.last("c"))
                    sp.dma_start(c_ctx[:, :], ctx_rows[rows(now.t - LAG["c"]), :]).then_inc(sem["c_loaded"], 16)
                if s == "e_o":
                    sp.wait_ge(sem["e_o.free"], now.done("e"))
                    sp.dma_start(out_rows[rows(now.t - LAG["e"]), :], e_out[:, :]).then_inc(sem["stored"], 16)

            run(sp, step)
            sp.wait_ge(sem["stored"], 16 * NB)

        @block.gpsimd
        def _(pool):
            pool.wait_ge(sem["setup_done"], 1)

            def rsqrt(now, s):
                pool.wait_ge(sem[f"{s}_mv_done"], now.done(s))
                nc.gpsimd.tensor_tensor(rstd[s][:, 0:1], mv[s][:, 1:2], c["eps"][:, 0:1], ALU.add).then_inc(sem[f"{s}_vareps_done"], 1)
                pool.wait_ge(sem[f"{s}_vareps_done"], now.done(s))
                pool.wait_ge(sem[f"{s}_xn_done"], now.last(s))
                nc.gpsimd.tensor_tensor(rstd[s][:, 1:2], rstd[s][:, 0:1], c["eps"][:, 1:2], ALU.pow).then_inc(sem[f"{s}_rstd_done"], 1)

            def key_blocks(now, s, made_by, step):
                pool.wait_ge(sem[f"{step}.free"], now.done(made_by))
                pool.wait_ge(sem[f"{s}_s.full"], now.group_last(made_by, 3))
                for m in range(KT):
                    last = nc.gpsimd.tensor_tensor(
                        kb[s][:, m], kt[s][:, m].unsqueeze(1).broadcast_to([P, E0, P]),
                        c["heads"].unsqueeze(2).broadcast_to([P, E0, P]), ALU.mult)
                last.then_inc(sem[f"{s}_kb_done"], 1)

            def step(now, s):
                if s in ("a_ln", "b_ln", "c_ln", "d_ln"):
                    rsqrt(now, s[0])
                if s == "c_ln":
                    pool.wait_ge(sem["c_x_done"], now.done("c"))
                    pool.wait_ge(sem["c_o.free"], now.last("c"))
                    nc.gpsimd.tensor_tensor(c_xb[:, :], c_x[:, :], gbc[:, :], ALU.add).then_inc(sem["c_xb_done"], 1)
                if s == "c_tr":
                    pool.wait_ge(sem["c_loaded"], now.arrived("c", 16))
                    pool.wait_ge(sem["c_av"], now.group_last("c", 3))
                    nc.gpsimd.tensor_tensor(v1["c"][:, :, 0:HD], c_ctx[:, :].rearrange("p (h i) -> p h i", h=H),
                                            ones[:, 0:HD].unsqueeze(1).broadcast_to([P, H, HD]), ALU.mult).then_inc(sem["c_v1_done"], 1)
                if s == "a_qk":
                    pool.wait_ge(sem["a_qk.free"], now.done("a"))
                    pool.wait_ge(sem["a_tr2.full"], now.last("a"))
                    nc.gpsimd.tensor_tensor(a_qk[:, :], a_c[:, :], a_s[:, :], ALU.add).then_inc(sem["a_rotated"], 1)
                if s == "c_qk":
                    key_blocks(now, "c", "c", s)
                if s == "d_qk":
                    pool.wait_ge(sem["c_o.free"], now.done("d"))
                    pool.wait_ge(sem["e_o.free"], now.last("d"))
                    nc.gpsimd.tensor_tensor(e_xb[:, :], d_x[:, :], gbo[:, :], ALU.add).then_inc(sem["e_xb_done"], 1)
                    key_blocks(now, "e", "d", s)

            run(pool, step)

        @block.scalar
        def _(act):
            act.wait_ge(sem["loaded"], 32)
            nc.scalar.activation(tg[:, :], c["g"], ACT.Tanh).then_inc(sem["setup_g"], 1)

            def copy(dst, src):
                return nc.scalar.activation(dst, src, ACT.Copy)

            def weigh(now, s):
                act.wait_ge(sem[f"{s}_two_done"], now.done(s))
                nc.scalar.activation(top[s]["e"][:, :], top[s]["mx"][:, 1:2], ACT.Exp, bias=top[s]["n"][:, 0:1]).then_inc(sem[f"{s}_e_done"], 1)

            def exps(now, s, g):
                act.wait_ge(sem[f"{s}_s.free"], now.group_done(s, g))
                part = sc[s][:, g % 2]
                nc.scalar.activation(part, part, ACT.Exp).then_inc(sem[f"{s}_exp"], 1)

            def keep_probs(now, s, g):
                act.wait_ge(sem[f"{s}_t.full"], now.group_done(s, g))
                act.wait_ge(sem[f"{s}_av"], now.group_done(s, g - 2))
                ins = copy(pt[s][:, g % 2], psum(f"{s}_t{g}").rearrange("p (h q) -> p h q", h=GH))
                ins.then_inc(sem[f"{s}_t.free"], 1)

            def keep_weighted(now, s):
                act.wait_ge(sem[f"{s}_av"], now.group_done(s, 3))
                act.wait_ge(sem[f"{s}_z1.full"], now.last(s))
                copy(z[s][:, :, :], psum(f"{s}_v0").rearrange("p (g q) -> p g q", g=NG)).then_inc(sem[f"{s}_z0.free"], 1)

            def projections(now, step, s, bq, bk, stage):
                act.wait_ge(sem[f"{step}.full"], now.done(stage))
                src = psum(step).rearrange("p (m q) -> p m q", m=2 * KT)
                act.wait_ge(sem[f"{s}_s.full"], now.group_last(stage, 3))
                for m in range(KT):
                    last = nc.scalar.activation(qt[s][:, m], src[:, m], ACT.Identity, bias=bq[:, m:m + 1], scale=SCALE)
                last.then_inc(sem[f"{s}_qt_done"], 1)
                act.wait_ge(sem[f"{s}_kb_done"], now.last(stage))
                for m in range(KT):
                    last = nc.scalar.activation(kt[s][:, m], src[:, KT + m], ACT.Identity, bias=bk[:, m:m + 1])
                last.then_inc(sem[f"{step}.free"], 1)

            def step(now, s):
                if s == "a_tr":
                    act.wait_ge(sem["a_tr.full"], now.done("a"))
                    act.wait_ge(sem["a_v.full"], now.last("a"))
                    copy(a_t[:, :, :], psum(s).rearrange("p (m q) -> p m q", m=2 * KT)).then_inc(sem["a_tr.free"], 1)
                if s == "a_v":
                    act.wait_ge(sem["a_v.full"], now.done("a"))
                    act.wait_ge(sem["a_o.full"], now.last("a"))
                    copy(a_v[:, :], psum(s)[:, 0:D]).then_inc(sem["a_v.free"], 1)
                if s == "a_tr2":
                    act.wait_ge(sem["a_tr2.full"], now.done("a"))
                    act.wait_ge(sem["a_r.full"], now.last("a"))
                    copy(a_qkt[:, :, :], psum(s).rearrange("p (m q) -> p m q", m=2 * KT)).then_inc(sem["a_tr2.free"], 1)
                if s == "b_tr":
                    act.wait_ge(sem["b_tr.full"], now.done("b"))
                    act.wait_ge(sem["b_m3.full"], now.last("b"))
                    copy(b_t[:, :, :], psum(s)[:, 0:D].rearrange("p (m q) -> p m q", m=KT)).then_inc(sem["b_tr.free"], 1)
                if s == "b_g":
                    weigh(now, "b")
                if s == "b_w":
                    act.wait_ge(sem["b_w.full"], now.done("b"))
                    act.wait_ge(sem["b_be.full"], now.last("b"))
                    copy(b_wtt[:, :], psum(s)[:, 0:P]).then_inc(sem["b_w.free"], 1)
                if s == "c_tr":
                    act.wait_ge(sem["c_tr.full"], now.done("c"))
                    act.wait_ge(sem["c_qk.full"], now.last("c"))
                    copy(c_t[:, :, :], psum(s).rearrange("p (m q) -> p m q", m=2 * KT)).then_inc(sem["c_tr.free"], 1)
                if s == "c_qk":
                    projections(now, "c_qk", "c", bq1s, c["bk1"], "c")
                if s[0] in "ce" and s[2] == "s":
                    exps(now, s[0], int(s[3]))
                if s[0] in "ce" and s[2] == "t" and s[3].isdigit():
                    keep_probs(now, s[0], int(s[3]))
                if s in ("c_z0", "e_z0"):
                    keep_weighted(now, s[0])
                if s == "c_yt":
                    act.wait_ge(sem["c_yt.full"], now.done("c"))
                    act.wait_ge(sem["c_o.full"], now.last("c"))
                    copy(yt["c"][:, :, :], psum(s)[:, 0:D].rearrange("p (m q) -> p m q", m=KT)).then_inc(sem["c_yt.free"], 1)
                if s == "e_yt":
                    act.wait_ge(sem["e_yt.full"], now.done("e"))
                    act.wait_ge(sem["e_o.full"], now.last("e"))
                    act.wait_ge(sem["e_bv_done"], now.done("e"))
                    for m in range(KT):
                        last = nc.scalar.activation(yt["e"][:, m], psum(s)[:, m * P:(m + 1) * P], ACT.Identity,
                                                    bias=e_bv[:, m:m + 1])
                    last.then_inc(sem["e_yt.free"], 1)
                if s == "d_tr":
                    act.wait_ge(sem["d_tr.full"], now.done("d"))
                    act.wait_ge(sem["d_v.full"], now.last("d"))
                    act.wait_ge(sem["d_h.full"], now.last("d"))
                    for m in range(KT):
                        last = nc.scalar.activation(d_t[:, m], psum(s)[:, m * P:(m + 1) * P], ACT.Copy,
                                                    accum_out=d_pool[:, m:m + 1])
                    last.then_inc(sem["d_tr.free"], 1)
                if s == "d_lg":
                    weigh(now, "d")
                if s in ("d_c0", "d_c1", "d_c2"):
                    j = int(s[3])
                    act.wait_ge(sem["d_w_done"], now.done("d"))
                    act.wait_ge(sem["d_v.full" if j == 2 else "d_qk.full"], now.last("d"))
                    nc.scalar.activation(d_wx[:, j], wx[:, 0, j * KT * D:(j + 1) * KT * D], ACT.Copy,
                                         scale=top["d"]["w"][:, 0:1]).then_inc(sem[f"d_c{j}_first"], 1)
                if s == "d_qk":
                    act.wait_ge(sem["d_bx_done"], now.done("d"))
                    projections(now, "d_qk", "e", d_bx, d_bx[:, KT:2 * KT], "d")
                if s == "d_v":
                    act.wait_ge(sem["d_v.full"], now.done("d"))
                    act.wait_ge(sem["e_av"], now.group_last("d", 3))
                    copy(v1["e"][:, :, 0:HD], psum(s)[:, 0:D].rearrange("p (h i) -> p h i", h=H)).then_inc(sem["d_v.free"], 1)

            run(act, step)

        @block.vector
        def _(dve):
            dve.wait_ge(sem["setup_g"], 1)
            dve.wait_ge(sem["loaded"], 32)
            nc.vector.tensor_scalar(gbc[:, :], c["bc1"], tg[:, 2:3], None, ALU.mult)
            nc.vector.tensor_scalar(gbo[:, :], c["bo"], tg[:, 3:4], None, ALU.mult)
            nc.vector.tensor_scalar(bq1s[:, :], c["bq1"], SCALE, None, ALU.mult)
            nc.vector.memset(ones[:, :], 1.0)
            nc.vector.memset(b_wt[:, :], 0.0)
            for s in "ce":
                nc.vector.memset(v1[s][:, :, HD:2 * HD], 1.0)
            nc.vector.memset(top["d"]["lg"][:, :], 0.0).then_inc(sem["setup_done"], 1)
            dve.wait_ge(sem["setup_done"], 1)

            def link(now, ins, event):
                ins.then_inc(sem[event], 1)
                dve.wait_ge(sem[event], now.done(event[0]))

            def carry_waits():
                nc.vector.memset(carrier[:, :], 0.0)

            def stats_of(now, s, src):
                link(now, nc.vector.bn_stats(stats[s][:, :], src), f"{s}_stats_done")
                dve.wait_ge(sem[f"{s}_vareps_done"], now.last(s))
                carry_waits()
                nc.vector.bn_aggr(mv[s][:, :], stats[s][:, :]).then_inc(sem[f"{s}_mv_done"], 1)

            def normalise(now, s, dst, src):
                dve.wait_ge(sem[f"{s}_rstd_done"], now.done(s))
                dve.wait_ge(sem[f"{s}_tr.full"], now.last(s))
                nc.vector.tensor_scalar(dst[:, :], src[:, :], mv[s][:, 0:1], rstd[s][:, 1:2], ALU.subtract,
                                        ALU.mult).then_inc(sem[f"{s}_xn_done"], 1)

            def rotate(now, step):
                dve.wait_ge(sem[f"{step}.full"], now.done("a"))
                dve.wait_ge(sem["a_rotated"], now.last("a"))
                src = psum(step)
                nc.vector.tensor_tensor(a_c[:, :], src[:, :], c["cos"], ALU.mult)
                pairs, out2, sin2 = (v.rearrange("p (i two) -> p i two", two=2) for v in (src[:, :], a_s[:, :], c["sin"]))
                nc.vector.tensor_tensor(out2[:, :, 0], pairs[:, :, 1], sin2[:, :, 0], ALU.mult)
                nc.vector.tensor_tensor(out2[:, :, 1], pairs[:, :, 0], sin2[:, :, 1], ALU.mult).then_inc(sem[f"{step}.free"], 1)

            def top_two(now, s, width, bias):
                step, it = {"b": "b_g", "d": "d_lg"}[s], top[s]
                dve.wait_ge(sem[f"{step}.full"], now.done(s))
                ins = nc.vector.tensor_tensor(it["lg"][:, :], psum(step)[:, 0:8], bias, ALU.add)
                ins.then_inc(sem[f"{step}.free"], 1)
                dve.wait_ge(sem[f"{step}.free"], now.done(s))
                dve.wait_ge(sem[f"{s}_e_done"], now.last(s))
                carry_waits()
                link(now, nc.vector.max(it["mx"][:, :], it["lg"][:, :]), f"{s}_max_done")
                nc.vector.tensor_scalar(it["n"][:, :], it["mx"][:, 0:1], -1.0, None, ALU.mult).then_inc(sem[f"{s}_two_done"], 1)
                link(now, nc.vector.max_index(it["ix"][:, :], it["mx"][:, :], it["lg"][:, :]), f"{s}_ix_done")
                link(now, nc.vector.tensor_copy(it["if"][:, :], it["ix"][:, 0:2]), f"{s}_if_done")

            def weights_of(now, s, dst):
                it = top[s]
                dve.wait_ge(sem[f"{s}_e_done"], now.done(s))
                link(now, nc.vector.tensor_scalar(it["s"][:, :], it["e"][:, :], 1.0, None, ALU.add), f"{s}_sum_done")
                link(now, nc.vector.reciprocal(it["r"][:, 0:1], it["s"][:, :]), f"{s}_first_done")
                link(now, nc.vector.tensor_tensor(it["r"][:, 1:2], it["r"][:, 0:1], it["e"][:, :], ALU.mult), f"{s}_second_done")
                nc.vector.tensor_scalar(it["w1"][:, :], c["iota"], it["if"][:, 0:1], it["r"][:, 0:1], ALU.is_equal, ALU.mult)
                link(now, nc.vector.tensor_scalar(it["w2"][:, :], c["iota"], it["if"][:, 1:2], it["r"][:, 1:2],
                                                  ALU.is_equal, ALU.mult), f"{s}_placed")
                return nc.vector.tensor_tensor(dst, it["w1"][:, :], it["w2"][:, :], ALU.add)

            def scores(now, s, g):
                dve.wait_ge(sem[f"{s}_s.full"], now.group_done(s, g))
                src = psum(f"{s}_s{g}").rearrange("p (h k) -> p h k", h=GH)
                m = mx[s][:, GH * g:GH * g + GH]
                nc.vector.tensor_reduce(m, src, axis=AX.X, op=ALU.max).then_inc(sem[f"{s}_max"], 1)
                dve.wait_ge(sem[f"{s}_max"], now.group_done(s, g))
                dve.wait_ge(sem[f"{s}_t.full"], now.group_done(s, g - 2))
                nc.vector.tensor_tensor(sc[s][:, g % 2], src, m.unsqueeze(2).broadcast_to([P, GH, P]),
                                        ALU.subtract).then_inc(sem[f"{s}_s.free"], 1)

            def weighted(now, s):
                dve.wait_ge(sem[f"{s}_z1.full"], now.done(s))
                heads = psum(f"{s}_z1").rearrange("p (h i) -> p h i", h=H)
                link(now, nc.vector.reciprocal(rz[s][:, :].unsqueeze(2), heads[:, :, HD:HD + 1]), f"{s}_rz_done")
                dve.wait_ge(sem[f"{s}_yt.full"], now.last(s))
                nc.vector.tensor_tensor(y[s][:, :].rearrange("p (h i) -> p h i", h=H), heads[:, :, 0:HD],
                                        rz[s][:, :].unsqueeze(2).broadcast_to([P, H, HD]), ALU.mult).then_inc(sem[f"{s}_z1.free"], 1)

            def gated(now, s, dst, residual, gate):
                return nc.vector.scalar_tensor_tensor(dst[:, :], psum(s)[:, 0:D], tg[:, gate:gate + 1], residual[:, :],
                                                      ALU.mult, ALU.add)

            def step(now, s):
                if s == "a_ln":
                    dve.wait_ge(sem["a_loaded"], now.arrived("a", 32))
                    stats_of(now, "a", a_x[:, :])
                if s == "b_ln":
                    dve.wait_ge(sem["a_o.free"], now.done("b"))
                    stats_of(now, "b", b_x[:, :])
                if s == "c_ln":
                    dve.wait_ge(sem["c_x_done"], now.done("c"))
                    stats_of(now, "c", c_x[:, :])
                if s == "d_ln":
                    dve.wait_ge(sem["c_o.free"], now.done("d"))
                    stats_of(now, "d", d_x[:, :])
                if s in ("a_tr", "b_tr", "c_tr", "d_tr"):
                    normalise(now, s[0], {"a": a_xn, "b": b_xn, "c": c_xn, "d": d_xn}[s[0]],
                              {"a": a_x, "b": b_x, "c": c_x, "d": d_x}[s[0]])
                if s == "a_qk":
                    rotate(now, s)
                if s == "a_r":
                    dve.wait_ge(sem["a_r.full"], now.done("a"))
                    dve.wait_ge(sem["a_o.full"], now.last("a"))
                    nc.vector.tensor_tensor(a_ret[:, :], psum(s)[:, 0:P], c["decay"], ALU.mult).then_inc(sem["a_r.free"], 1)
                if s == "a_o":
                    dve.wait_ge(sem["a_o.full"], now.done("a"))
                    dve.wait_ge(sem["c_x_done"], now.last("a"))
                    gated(now, s, b_x, a_x, 0).then_inc(sem["a_o.free"], 1)
                if s == "b_g":
                    top_two(now, "b", E0, c["bgate"])
                if s == "b_w":
                    dve.wait_ge(sem["b_w.full"], now.last("b"))
                    weights_of(now, "b", b_wt[:, 0:8]).then_inc(sem["b_wt_done"], 1)
                if s == "b_be":
                    dve.wait_ge(sem["b_be.full"], now.done("b"))
                    nc.vector.tensor_copy(b_acc[:, :], psum(s)[:, 0:D]).then_inc(sem["b_be.free"], 1)
                if s in ("b_m0", "b_m1", "b_m2", "b_m3"):
                    j = int(s[3])
                    dve.wait_ge(sem[f"{s}.full"], now.done("b"))
                    dve.wait_ge(sem["b_be.free" if j == 0 else f"b_m{j - 1}.free"], now.done("b"))
                    for i in range(2):
                        e = 2 * j + i
                        ins = nc.vector.scalar_tensor_tensor(b_acc[:, :], psum(s)[:, i * D:(i + 1) * D], b_wt[:, e:e + 1],
                                                             b_acc[:, :], ALU.mult, ALU.add)
                        if i == 0:
                            link(now, ins, f"b_half{j}")
                    ins.then_inc(sem[f"{s}.free"], 1)
                    if j == 3:
                        dve.wait_ge(sem["b_m3.free"], now.done("b"))
                        dve.wait_ge(sem["c_xb_done"], now.last("b"))
                        nc.vector.scalar_tensor_tensor(c_x[:, :], b_acc[:, :], tg[:, 1:2], b_x[:, :], ALU.mult,
                                                       ALU.add).then_inc(sem["c_x_done"], 1)
                if s[0] in "ce" and s[2] == "s":
                    scores(now, s[0], int(s[3]))
                if s in ("c_z1", "e_z1"):
                    weighted(now, s[0])
                if s == "c_o":
                    dve.wait_ge(sem["c_o.full"], now.done("c"))
                    dve.wait_ge(sem["c_xb_done"], now.done("c"))
                    dve.wait_ge(sem["e_xb_done"], now.last("c"))
                    gated(now, s, d_x, c_xb, 2).then_inc(sem["c_o.free"], 1)
                if s == "e_o":
                    dve.wait_ge(sem["e_o.full"], now.done("e"))
                    dve.wait_ge(sem["e_xb_done"], now.done("e"))
                    dve.wait_ge(sem["stored"], now.count(16, -16 * LAG["e"]))
                    gated(now, s, e_out, e_xb, 3).then_inc(sem["e_o.free"], 1)
                if s == "d_h":
                    dve.wait_ge(sem["d_h.full"], now.done("d"))
                    ins = nc.vector.tensor_scalar(d_h[:, :], psum(s)[:, 0:1], 1.0 / P, c["bh"], ALU.mult, ALU.add)
                    ins.then_inc(sem["d_h.free"], 1)
                    dve.wait_ge(sem["d_h.free"], now.done("d"))
                    dve.wait_ge(sem["d_lg.full"], now.last("d"))
                    nc.vector.tensor_scalar(d_hb[:, :], ones[:, :], d_h[:, 0:1], 0.0, ALU.mult, ALU.max).then_inc(sem["d_hb_done"], 1)
                if s == "d_lg":
                    top_two(now, "d", E1, c["bl"])
                if s == "d_w":
                    dve.wait_ge(sem["d_c2_first"], now.last("d"))
                    ins = weights_of(now, "d", top["d"]["w"][:, :])
                    ins.then_inc(sem["d_w_done"], 1)
                    dve.wait_ge(sem["d_w_done"], now.done("d"))
                    dve.wait_ge(sem["d_qk.free"], now.last("d"))
                    w = top["d"]["w"]
                    link(now, nc.vector.tensor_scalar(d_bx[:, :], bx[:, 0], w[:, 0:1], None, ALU.mult), "d_bx0")
                    for e in range(1, E1):
                        link(now, nc.vector.scalar_tensor_tensor(d_bx[:, :], bx[:, e], w[:, e:e + 1], d_bx[:, :], ALU.mult,
                                                                 ALU.add), f"d_bx{e}")
                    nc.vector.tensor_scalar(d_bx[:, 0:KT], d_bx[:, 0:KT], SCALE, None, ALU.mult).then_inc(sem["d_bx_done"], 1)
                if s in ("d_c0", "d_c1", "d_c2"):
                    j = int(s[3])
                    dve.wait_ge(sem[f"d_c{j}_first"], now.done("d"))
                    w, n = top["d"]["w"], KT * D
                    for e in range(1, E1):
                        ins = nc.vector.scalar_tensor_tensor(d_wx[:, j], wx[:, e, j * n:(j + 1) * n], w[:, e:e + 1], d_wx[:, j],
                                                             ALU.mult, ALU.add)
                        if e < E1 - 1:
                            link(now, ins, f"d_c{j}_{e}")
                        else:
                            ins.then_inc(sem[f"d_c{j}_done"], 1)
                    if j == 2:
                        dve.wait_ge(sem["e_yt.free"], now.last("d"))
                        nc.vector.tensor_copy(e_bv[:, :], d_bx[:, 2 * KT:3 * KT]).then_inc(sem["e_bv_done"], 1)

            run(dve, step)

        @block.tensor
        def _(pe):
            pe.wait_ge(sem["loaded"], 32)
            pe.wait_ge(sem["setup_done"], 1)

            def mm(dst, lhs, rhs, k=0, last=0):
                return nc.tensor.matmul(dst, lhs, rhs, start=k == 0, stop=k == last)

            def transposes(s, tiles):
                out = psum(s).rearrange("p (m q) -> p m q", m=2 * KT)
                for m, tile in enumerate(tiles):
                    ins = nc.tensor.transpose(out[:, m], tile, ident)
                return ins

            def halves(tile):
                return [tile[:, m * P:(m + 1) * P] for m in range(KT)]

            def by_tokens(s, lhs, rhs, n, at=0):
                for k in range(KT):
                    ins = mm(psum(s)[:, at:at + n], lhs[:, k], rhs[:, k], k, KT - 1)
                return ins

            def by_channels(s, at, w, rhs):
                for m in range(KT):
                    for k in range(KT):
                        ins = mm(psum(s)[:, (at + m) * P:(at + m + 1) * P], w[:, k, m * P:(m + 1) * P], rhs[:, k], k, KT - 1)
                return ins

            def attention(now, s, step):
                g = int(step[3])
                if step[2] == "s":
                    made_by = "d" if s == "e" else "c"
                    if g == 0:
                        pe.wait_ge(sem[f"{s}_qt_done"], now.done(s))
                        pe.wait_ge(sem[f"{s}_kb_done"], now.done(s))
                    m, at = g * GH // E0, g * GH % E0
                    mm(psum(step).rearrange("p (h k) -> p h k", h=GH), qt[s][:, m], kb[s][:, m, at:at + GH]).then_inc(sem[f"{s}_s.full"], 1)
                elif step[2] == "t":
                    pe.wait_ge(sem[f"{s}_exp"], now.group_done(s, g))
                    transposes(step, [sc[s][:, g % 2, j] for j in range(GH)]).then_inc(sem[f"{s}_t.full"], 1)
                else:
                    pe.wait_ge(sem[f"{s}_t.free"], now.group_done(s, g))
                    if g == 0:
                        pe.wait_ge(sem[f"{s}_v1_done" if s == "c" else "d_v.free"], now.done(s))
                    for j in range(GH):
                        ins = nc.tensor.matmul(psum(step)[32 * j:32 * j + 32, g * P:(g + 1) * P], v1[s][:, GH * g + j],
                                               pt[s][:, g % 2, j], start=True, stop=True, tile_position=(0, 32 * j))
                    ins.then_inc(sem[f"{s}_av"], 1)

            def step(now, s):
                if TAKES[s]:
                    pe.wait_ge(sem[now.reader(s)], now.released(s))
                heads = s in GROUPED
                full = sem[f"{s}.full"] if TAKES[s] and not heads else None
                if s == "a_tr":
                    pe.wait_ge(sem["a_xn_done"], now.done("a"))
                    transposes(s, halves(a_xn) + halves(a_ctx)).then_inc(full, 1)
                if s == "a_qk":
                    pe.wait_ge(sem["a_tr.free"], now.done("a"))
                    by_tokens(s, a_t[:, 0:KT], wq0, D)
                    by_tokens(s, a_t[:, KT:2 * KT], wk0, D, at=D).then_inc(full, 1)
                if s == "a_v":
                    by_tokens(s, a_t[:, KT:2 * KT], wv0, D).then_inc(full, 1)
                if s == "a_tr2":
                    pe.wait_ge(sem["a_rotated"], now.done("a"))
                    transposes(s, halves(a_qk[:, 0:D]) + halves(a_qk[:, D:2 * D])).then_inc(full, 1)
                if s == "a_r":
                    pe.wait_ge(sem["a_tr2.free"], now.done("a"))
                    for k in range(KT):
                        ins = mm(psum(s)[:, 0:P], a_qkt[:, KT + k], a_qkt[:, k], k, KT - 1)
                    ins.then_inc(full, 1)
                if s == "a_o":
                    pe.wait_ge(sem["a_r.free"], now.done("a"))
                    mm(psum(s)[:, 0:D], a_ret[:, :], a_v[:, :]).then_inc(full, 1)
                if s == "b_tr":
                    pe.wait_ge(sem["b_xn_done"], now.done("b"))
                    transposes(s, halves(b_xn)).then_inc(full, 1)
                if s == "b_g":
                    pe.wait_ge(sem["b_tr.free"], now.done("b"))
                    by_tokens(s, b_t, wgate, P).then_inc(full, 1)
                if s == "b_w":
                    pe.wait_ge(sem["b_wt_done"], now.done("b"))
                    nc.tensor.transpose(psum(s)[:, 0:P], b_wt[:, :], ident).then_inc(full, 1)
                if s == "b_be":
                    pe.wait_ge(sem["b_w.free"], now.done("b"))
                    mm(psum(s)[:, 0:D], b_wtt[:, :], c["be"]).then_inc(full, 1)
                if s in ("b_m0", "b_m1", "b_m2", "b_m3"):
                    j = int(s[3])
                    by_tokens(s, b_t, we[:, :, 2 * j * D:2 * (j + 1) * D], 2 * D).then_inc(full, 1)
                if s == "c_tr":
                    pe.wait_ge(sem["c_xn_done"], now.done("c"))
                    pe.wait_ge(sem["c_loaded"], now.arrived("c", 16))
                    transposes(s, halves(c_xn) + halves(c_ctx)).then_inc(full, 1)
                if s == "c_qk":
                    pe.wait_ge(sem["c_tr.free"], now.done("c"))
                    by_channels(s, 0, wq1, c_t[:, 0:KT])
                    by_channels(s, KT, wk1, c_t[:, KT:2 * KT]).then_inc(full, 1)
                if s == "d_tr":
                    pe.wait_ge(sem["d_xn_done"], now.done("d"))
                    transposes(s, halves(d_xn)).then_inc(full, 1)
                if s == "d_h":
                    pe.wait_ge(sem["d_tr.free"], now.done("d"))
                    for k in range(KT):
                        ins = mm(psum(s)[:, 0:1], wh[:, k], d_pool[:, k:k + 1], k, KT - 1)
                    ins.then_inc(full, 1)
                if s == "d_lg":
                    pe.wait_ge(sem["d_hb_done"], now.done("d"))
                    mm(psum(s)[:, 0:8], d_hb[:, :], c["wl"]).then_inc(full, 1)
                if s == "d_qk":
                    pe.wait_ge(sem["d_c0_done"], now.done("d"))
                    by_channels(s, 0, d_wx[:, 0].rearrange("p (k n) -> p k n", k=KT), d_t)
                    pe.wait_ge(sem["d_c1_done"], now.done("d"))
                    by_channels(s, KT, d_wx[:, 1].rearrange("p (k n) -> p k n", k=KT), d_t).then_inc(full, 1)
                if s == "d_v":
                    pe.wait_ge(sem["d_c2_done"], now.done("d"))
                    by_tokens(s, d_t, d_wx[:, 2].rearrange("p (k n) -> p k n", k=KT), D).then_inc(full, 1)
                if heads:
                    attention(now, s[0], s)
                if s in ("c_z1", "e_z1"):
                    pe.wait_ge(sem[f"{s[0]}_z0.free"], now.done(s[0]))
                    transposes(s, [z[s[0]][:, g] for g in range(NG)]).then_inc(full, 1)
                if s in ("c_yt", "e_yt"):
                    pe.wait_ge(sem[f"{s[0]}_z1.free"], now.done(s[0]))
                    transposes(s, halves(y[s[0]])).then_inc(full, 1)
                if s in ("c_o", "e_o"):
                    pe.wait_ge(sem[f"{s[0]}_yt.free"], now.done(s[0]))
                    by_tokens(s, yt[s[0]], wc1 if s[0] == "c" else wo, D).then_inc(full, 1)

            run(pe, step)


def shape_tables():
    f = np.float32
    base = (np.arange(0, D, 2, dtype=f) + f(0.4 * D)) / f(1.4 * D)
    pos = np.arange(P, dtype=f)
    scale = base[None, :] ** (pos[:, None] / f(512.0))
    freqs = f(1.0) / f(10000.0) ** (np.arange(D // 2, dtype=f) / f(D // 2))
    angle = pos[:, None] * freqs[None, :]
    sign = np.tile(np.array([-1.0, 1.0], f), D // 2)

    def twice(a):
        return np.repeat(a, 2, axis=1).astype(f)

    u, v = np.arange(P)[None, :], np.arange(P)[:, None]
    decay = np.where(u >= v, f(GAMMA) ** np.maximum(u - v, 0).astype(f), f(0))
    heads = (np.arange(P)[:, None] // HD == np.arange(E0)[None, :])
    rows = {
        "cos": np.concatenate([twice(np.cos(angle) * s) for s in (scale, f(1) / scale)], axis=1),
        "sin": np.concatenate([twice(np.sin(angle) * s) * sign for s in (scale, f(1) / scale)], axis=1),
        "decay": decay, "ident": np.eye(P), "heads": heads, "iota": np.tile(np.arange(E0), (P, 1)),
        "eps": np.tile(np.array([EPS, -0.5]), (P, 1)),
    }
    return np.concatenate([rows[name].astype(f).reshape(P, n) for name, n in TABLES], axis=1)


def laid_out(i):
    def tiles(w):
        return w.reshape(KT, P, -1).transpose(1, 0, 2).reshape(P, -1)

    def everywhere(v, n=None):
        v = v.reshape(1, -1)
        return np.broadcast_to(v, (P, v.shape[1]))

    def columns(v):
        return v.reshape(KT, P).T

    def wider(w, rows, cols, fill=0.0):
        out = np.full((rows, cols), fill, np.float32)
        out[:w.shape[0], :w.shape[1]] = w
        return out

    mixed = np.stack([i["L1_ffn_Wq"], i["L1_ffn_Wk"], i["L1_ffn_Wv"]], axis=1).reshape(E1, 3, KT, P, D)
    mixed_b = np.stack([i["L1_ffn_bq"], i["L1_ffn_bk"], i["L1_ffn_bv"]], axis=1).reshape(E1, 3, KT, P)
    gates = np.stack([i["g_xattn"][0], i["g_ffn"][0], i["g_xattn"][1], i["g_ffn"][1]])
    parts = {
        "wq0": tiles(i["L0_xattn_Wq"].T),
        "wk0": tiles(i["L0_xattn_Wk"].T), "wv0": tiles(i["L0_xattn_Wv"].T),
        "we": tiles(i["L0_ffn_We"].transpose(2, 0, 1).reshape(D, E0 * D)),
        "be": wider(i["L0_ffn_be"], P, D), "wgate": tiles(wider(i["L0_ffn_Wg"], D, P)), "bgate": everywhere(i["L0_ffn_bg"]),
        "wq1": tiles(i["L1_xattn_Wq"].T), "wk1": tiles(i["L1_xattn_Wk"].T), "bq1": columns(i["L1_xattn_bq"]),
        "bk1": columns(i["L1_xattn_bk"]), "wc1": tiles(i["L1_xattn_Wc"].T), "bc1": everywhere(i["L1_xattn_bc"]),
        "wx": mixed.transpose(3, 0, 1, 2, 4).reshape(P, -1), "bx": mixed_b.transpose(3, 0, 1, 2).reshape(P, -1),
        "wh": tiles(i["L1_ffn_Wg1"]), "bh": i["L1_ffn_bg1"].reshape(P, 1), "wl": wider(i["L1_ffn_Wg2"], P, E0),
        "bl": everywhere(wider(i["L1_ffn_bg2"].reshape(1, E1), 1, E0, NEG)), "wo": tiles(i["L1_ffn_Wo"]),
        "bo": everywhere(i["L1_ffn_bo"]), "g": everywhere(gates),
    }
    return np.ascontiguousarray(np.concatenate([parts[name].reshape(P, n) for name, n in WEIGHTS], axis=1))


def kernel(**inputs):
    import concourse.bacc as bacc
    from concourse.bass_utils import run_bass_kernel_spmd

    i = {name: np.asarray(a) for name, a in inputs.items()}
    arrays = {"x": np.ascontiguousarray(i["x"]), "ctx": np.ascontiguousarray(i["ctx_1024"]), "weights": laid_out(i),
              "tables": shape_tables()}
    nc = bacc.Bacc("TRN2", target_bir_lowering=False, num_devices=1)
    aps = [nc.dram_tensor(name, a.shape, F32, kind="ExternalInput").ap() for name, a in arrays.items()]
    out = nc.dram_tensor("out", (NB, P, D), F32, kind="ExternalOutput").ap()
    build(nc, *aps, out)
    result = run_bass_kernel_spmd(nc, [arrays], core_ids=[0])
    return result.results[0]["out"]
```

```python
import numpy as np
import concourse.bass as bass
from concourse import mybir
from contextlib import ExitStack

F32 = mybir.dt.float32
F32R = mybir.dt.float32r
U32 = mybir.dt.uint32
ALU = mybir.AluOpType
ACT = mybir.ActivationFunctionType
AX = mybir.AxisListType

NB = 32
P = 128
D = 256
KT = D // P
H = 16
HD = D // H
NG = 4
GH = H // NG
E0 = 8
E1 = 4
GAMMA = 0.96875
EPS = 1e-5
SCALE = 1.0 / float(np.sqrt(HD))
BY_DVE = "c"
NEG = -3.0e38

LAG = {"a": 0, "b": 1, "c": 2, "d": 3, "e": 4}
DEPTH = max(LAG.values())
UNROLL = 3

ORDERS = {
    "pe": """
        e_s0 c_tr d_tr e_s1 b_tr d_h c_qk d_lg b_g e_t0 a_tr e_s2 e_t1 e_v0 a_qk e_v1 e_t2 b_w c_s0 b_be e_s3
        a_v c_s1 e_v2 b_m0 e_t3 c_t0 c_s2 e_v3 b_m1 c_t1 a_tr2 c_s3 c_v0 e_z1 c_t2 b_m2 c_v1 c_t3 e_yt d_qk c_v2
        c_v3 e_o a_r c_z1 b_m3 c_yt a_o c_o d_v
    """.split(),
    "dve": """
        c_st d_st c_ag b_st d_ag e_m0 c_nm b_ag d_nm a_st b_nm a_ag e_m1 a_nm d_h d_hb d_g0 b_g0 d_g1 d_g2 b_g1
        b_g2 b_w0 d_w0 b_w1 b_w2 d_g3 d_w1 b_g3 e_m2 d_w2 b_w3 d_w3 d_w4 d_b0 b_w4 a_qk c_m0 c_s0 d_c0a b_be
        e_m3 c_m1 c_s1 b_m0a d_c1a b_m0b d_c1b c_m2 c_s2 d_c0b d_b1 b_m1a d_b2 b_m1b c_m3 e_rz c_s3 d_c0c e_y
        d_b3 d_c1c b_m2a b_m2b d_c2a d_c2b d_c2c a_r c_rz c_y d_bv e_o b_m3a b_m3b b_fin a_o c_o
    """.split(),
    "act": """
        e_s0 c_tr d_tr b_tr e_s1 c_qk d_lg e_t0 b_g a_tr e_t1 e_s2 b_w e_t2 d_c0 b_hi d_c2 c_s0 d_c1 e_s3 c_s1
        e_t3 c_t0 a_v c_s2 e_z0 c_t1 c_t2 c_s3 a_tr2 e_yt c_t3 d_qk c_z0 c_yt d_v
    """.split(),
    "pool": """
        c_ve c_rs d_ve d_rs b_ve b_rs a_ve c_xb a_rs c_kb b_lo a_qk c_v1 d_kb d_xb
    """.split(),
    "sp": """
        c_in a_in e_out
    """.split(),
}
BANK = {
    "a_tr": "M0", "a_qk": "M0", "a_v": "M0", "a_tr2": "M0", "a_r": "M0", "a_o": "M0",
    "b_tr": "M1", "b_g": "M1", "b_w": "M1", "b_be": "M1", "b_m0": "M1", "b_m1": "M1", "b_m2": "M1", "b_m3": "M1",
    "c_tr": "TC", "c_qk": "SC", "c_z1": "SC", "c_yt": "TC", "c_o": "ZC", "c_v": "ZC",
    "d_tr": "M0", "d_h": "M0", "d_lg": "M0", "d_qk": "SE", "d_v": "TE",
    "e_z1": "SE", "e_yt": "TE", "e_o": "ZE", "e_v": "ZE",
}
for _g in range(NG):
    BANK[f"c_s{_g}"], BANK[f"e_s{_g}"] = "SC", "SE"
    BANK[f"c_t{_g}"], BANK[f"e_t{_g}"] = "TC", "TE"
TAKES = {s: (BANK["c_v"] if s[0] == "c" else BANK["e_v"]) if s[2:] == "v0" else BANK.get(s) for s in ORDERS["pe"]}


GROUPED = {s for s in ORDERS["pe"] if s[0] in "ce" and s[2] in "stv" and s[3].isdigit()}


def before(bank, step, t):
    users = [s for s in ORDERS["pe"] if TAKES[s] == bank]
    at = users.index(step)
    for back in range(1, len(users) * (DEPTH + 2) + 1):
        user, turns = users[(at - back) % len(users)], (at - back) // len(users)
        batch = t - LAG[user[0]] + turns
        if not isinstance(t, int) or 0 <= batch < NB:
            return user, batch
    return None


WEIGHTS = [
    ("wq0", KT * D), ("wk0", KT * D), ("wv0", KT * D), ("we", KT * E0 * D), ("be", D), ("wgate", KT * P), ("bgate", E0),
    ("wq1", KT * D), ("wk1", KT * D), ("bq1", KT), ("bk1", KT), ("wc1", KT * D), ("bc1", D),
    ("wx", E1 * 3 * KT * D), ("bx", E1 * 3 * KT), ("wh", KT * P), ("bh", 1), ("wl", E0), ("bl", E0),
    ("wo", KT * D), ("bo", D), ("g", 4),
]
TABLES = [
    ("cos", 2 * D), ("sin", 2 * D), ("decay", P), ("ident", P), ("heads", E0), ("iota", E0), ("eps", 2),
]


def build(nc, x, ctx_in, weights, tables, out):
    with ExitStack() as stack:
        def sb(name, *shape, dt=F32):
            return stack.enter_context(nc.sbuf_tensor(name, [P, *shape], dt))

        wsum, tsum = sum(n for _, n in WEIGHTS), sum(n for _, n in TABLES)
        w_sb, t_sb = sb("w_sb", wsum), sb("t_sb", tsum)
        c = {}
        for tile, parts in ((w_sb, WEIGHTS), (t_sb, TABLES)):
            at = 0
            for name, n in parts:
                c[name] = tile[:, at:at + n]
                at += n
        wq0 = c["wq0"].rearrange("p (k n) -> p k n", k=KT)
        wk0 = c["wk0"].rearrange("p (k n) -> p k n", k=KT)
        wv0 = c["wv0"].rearrange("p (k n) -> p k n", k=KT)
        we_h, we_l = sb("we_h", KT * E0 * D, dt=F32R), sb("we_l", KT * E0 * D, dt=F32R)
        we_hi, we_lo = (w[:, :].rearrange("p (k n) -> p k n", k=KT) for w in (we_h, we_l))
        wgate = c["wgate"].rearrange("p (k n) -> p k n", k=KT)
        wq1 = c["wq1"].rearrange("p (k n) -> p k n", k=KT)
        wk1 = c["wk1"].rearrange("p (k n) -> p k n", k=KT)
        wc1 = c["wc1"].rearrange("p (k n) -> p k n", k=KT)
        wx = c["wx"].rearrange("p (e n) -> p e n", e=E1)
        bx = c["bx"].rearrange("p (e n) -> p e n", e=E1)
        wh = c["wh"].rearrange("p (k n) -> p k n", k=KT)
        wo = c["wo"].rearrange("p (k n) -> p k n", k=KT)
        ident = c["ident"]

        tg = sb("tg", 4)
        gbc, gbo = sb("gbc", D), sb("gbo", D)
        bq1s = sb("bq1s", KT)
        ones, carrier = sb("ones", P), sb("carrier", 6)

        a_x, a_ctx, a_xn = sb("a_x", D), sb("a_ctx", D), sb("a_xn", D)
        a_t, a_qk, a_qkt = sb("a_t", 2 * KT, P), sb("a_qk", 2 * D), sb("a_qkt", 2 * KT, P)
        a_c, a_s = sb("a_c", 2 * D), sb("a_s", 2 * D)
        a_v, a_ret = sb("a_v", D), sb("a_ret", P)
        b_x, b_xn, b_t = sb("b_x", D), sb("b_xn", D), sb("b_t", KT, P)
        b_th, b_tl = sb("b_th", KT, P, dt=F32R), sb("b_tl", KT, P, dt=F32R)
        b_wt, b_wtt, b_acc = sb("b_wt", P), sb("b_wtt", P), sb("b_acc", D)
        c_x, c_xb, c_xn, c_ctx, c_t = sb("c_x", D), sb("c_xb", D), sb("c_xn", D), sb("c_ctx", D), sb("c_t", 2 * KT, P)
        d_x, d_xn, d_t, d_pool = sb("d_x", D), sb("d_xn", D), sb("d_t", KT, P), sb("d_pool", KT)
        d_h, d_hb = sb("d_h", 1), sb("d_hb", P)
        d_wx, d_bx = sb("d_wx", 3, KT * D), sb("d_bx", 3 * KT)
        e_xb, e_out, e_bv = sb("e_xb", D), sb("e_out", D), sb("e_bv", KT)
        stats = {s: sb(f"{s}_stats", 6) for s in "abcd"}
        mv = {s: sb(f"{s}_mv", 2) for s in "abcd"}
        rstd = {s: sb(f"{s}_rstd", 2) for s in "abcd"}
        top = {s: {"lg": sb(f"{s}_lg", 8), "mx": sb(f"{s}_mx", 8), "ix": sb(f"{s}_ix", 8, dt=U32), "if": sb(f"{s}_if", 2),
                   "n": sb(f"{s}_n", 1), "e": sb(f"{s}_e", 1), "s": sb(f"{s}_s", 1), "r": sb(f"{s}_r", 2),
                   "w1": sb(f"{s}_w1", 8), "w2": sb(f"{s}_w2", 8), "w": sb(f"{s}_wts", 8)} for s in "bd"}
        qt = {s: sb(f"{s}_qt", KT, P) for s in "ce"}
        kt = {s: sb(f"{s}_kt", KT, P) for s in "ce"}
        kb = {s: sb(f"{s}_kb", KT, E0, P) for s in "ce"}
        v1 = {s: sb(f"{s}_v1", H, 2 * HD) for s in "ce"}
        mx = {s: sb(f"{s}_smx", H) for s in "ce"}
        sc = {s: sb(f"{s}_sc", 2, GH, P) for s in "ce"}
        pt = {s: sb(f"{s}_pt", 2, GH, P) for s in "ce"}
        z = {s: sb(f"{s}_z", NG, P) for s in "ce"}
        rz = {s: sb(f"{s}_rz", H) for s in "ce"}
        y = {s: sb(f"{s}_y", D) for s in "ce"}
        yt = {s: sb(f"{s}_yt", KT, P) for s in "ce"}

        bank = {n: stack.enter_context(nc.psum_tensor(n, [P, 512], F32)) for n in ("M0", "M1", "SC", "TC", "ZC", "SE", "TE", "ZE")}

        def psum(step):
            return bank[BANK[step[:3] if step[2] == "v" and step[0] in "ce" else step]][:, :]

        class Semaphores(dict):

            def __missing__(self, event):
                self[event] = stack.enter_context(nc.semaphore(event.replace(".", "_")))
                return self[event]

        sem = Semaphores()

        block = stack.enter_context(nc.Block())

        class Turn:

            def __init__(self, eng, t, ahead):
                self.eng, self.t, self.ahead, self.counts = eng, t, ahead, {}

            def count(self, per, n):
                if isinstance(self.t, int):
                    return max(self.t * per + n, 0)
                if (per, n) not in self.counts:
                    self.counts[per, n] = self.eng.snap(self.t * (UNROLL * per) + (self.ahead * per + n))
                return self.counts[per, n]

            def done(self, stage):
                return self.count(1, 1 - LAG[stage])

            def last(self, stage):
                return self.count(1, -LAG[stage])

            def group_done(self, stage, g):
                return self.count(NG, -NG * LAG[stage] + g + 1)

            def group_last(self, stage, g):
                return self.count(NG, -NG * LAG[stage] + g + 1 - NG)

            def arrived(self, stage, each):
                return self.count(each, (1 - LAG[stage]) * each)

            def user(self, step):
                if isinstance(self.t, int):
                    return before(TAKES[step], step, self.t) or (step, -1)
                users = [s for s in ORDERS["pe"] if TAKES[s] == TAKES[step]]
                at = users.index(step)
                return users[at - 1], -LAG[users[at - 1][0]] - (at == 0)

            def reader(self, step):
                user, _ = self.user(step)
                if user[2:] == "v0":
                    return user[0] + "_z0.free"
                return user[:3] + ".free" if user in GROUPED else user + ".free"

            def released(self, step):
                user, batch = self.user(step)
                per, n = (NG, int(user[3]) + 1) if user in GROUPED and user[2] != "v" else (1, 1)
                if isinstance(self.t, int):
                    return max(batch * per + n, 0)
                return self.count(per, batch * per + n)

        def run(eng, order, step_fn):
            def turn(t, steps, ahead=0):
                now = Turn(eng, t, ahead)
                for s in steps:
                    step_fn(now, s)
            for t in range(DEPTH + 1):
                turn(t, [s for s in order if t >= LAG[s[0]]])
            with eng.Fori(0, (NB - DEPTH - 1) // UNROLL) as n:
                for ahead in range(UNROLL):
                    turn(n, order, DEPTH + 1 + ahead)
            for t in range(NB, NB + DEPTH):
                turn(t, [s for s in order if t - LAG[s[0]] < NB])

        x_rows = x.rearrange("b p d -> (b p) d")
        ctx_rows = ctx_in.rearrange("b p d -> (b p) d")
        out_rows = out.rearrange("b p d -> (b p) d")

        @block.sync
        def _(sp):
            sp.dma_start(t_sb[:, :], tables).then_inc(sem["loaded"], 16)
            sp.dma_start(w_sb[:, :], weights).then_inc(sem["loaded"], 16)

            def rows(now, lag):
                if isinstance(now.t, int):
                    return bass.ds((now.t - lag) * P, P)
                return bass.ds(now.t * (UNROLL * P) + (now.ahead - lag) * P, P)

            def step(now, s):
                if s == "a_in":
                    sp.wait_ge(sem["a_o.free"], now.last("a"))
                    sp.wait_ge(sem["a_tr.full"], now.last("a"))
                    sp.dma_start(a_x[:, :], x_rows[rows(now, 0), :]).then_inc(sem["a_loaded"], 16)
                    sp.dma_start(a_ctx[:, :], ctx_rows[rows(now, 0), :]).then_inc(sem["a_loaded"], 16)
                if s == "c_in":
                    sp.wait_ge(sem["c_tr.full"], now.last("c"))
                    sp.wait_ge(sem["c_v1_done"], now.last("c"))
                    sp.dma_start(c_ctx[:, :], ctx_rows[rows(now, LAG["c"]), :]).then_inc(sem["c_loaded"], 16)
                if s == "e_out":
                    sp.wait_ge(sem["e_o.free"], now.done("e"))
                    sp.dma_start(out_rows[rows(now, LAG["e"]), :], e_out[:, :]).then_inc(sem["stored"], 16)

            run(sp, ORDERS["sp"], step)
            sp.wait_ge(sem["stored"], 16 * NB)

        @block.gpsimd
        def _(pool):
            pool.wait_ge(sem["setup_done"], 1)

            def key_blocks(now, s, made_by, step):
                pool.wait_ge(sem[f"{step}.free"], now.done(made_by))
                pool.wait_ge(sem[f"{s}_s.full"], now.group_last(made_by, 3))
                for m in range(KT):
                    last = nc.gpsimd.tensor_tensor(
                        kb[s][:, m], kt[s][:, m].unsqueeze(1).broadcast_to([P, E0, P]),
                        c["heads"].unsqueeze(2).broadcast_to([P, E0, P]), ALU.mult)
                last.then_inc(sem[f"{s}_kb_done"], 1)

            def step(now, s):
                if s in ("a_ve", "b_ve", "c_ve", "d_ve"):
                    pool.wait_ge(sem[f"{s[0]}_mv_done"], now.done(s[0]))
                    nc.gpsimd.tensor_tensor(rstd[s[0]][:, 0:1], mv[s[0]][:, 1:2], c["eps"][:, 0:1], ALU.add).then_inc(sem[f"{s[0]}_vareps_done"], 1)
                if s in ("a_rs", "b_rs", "c_rs", "d_rs"):
                    pool.wait_ge(sem[f"{s[0]}_vareps_done"], now.done(s[0]))
                    pool.wait_ge(sem[f"{s[0]}_xn_done"], now.last(s[0]))
                    nc.gpsimd.tensor_tensor(rstd[s[0]][:, 1:2], rstd[s[0]][:, 0:1], c["eps"][:, 1:2], ALU.pow).then_inc(sem[f"{s[0]}_rstd_done"], 1)
                if s == "b_lo":
                    pool.wait_ge(sem["b_hi_done"], now.done("b"))
                    pool.wait_ge(sem["b_m3.full"], now.last("b"))
                    nc.gpsimd.tensor_tensor(b_tl[:, :, :], b_t[:, :, :], b_th[:, :, :].bitcast(F32), ALU.subtract).then_inc(sem["b_lo_done"], 1)
                if s == "c_xb":
                    pool.wait_ge(sem["c_x_done"], now.done("c"))
                    pool.wait_ge(sem["c_o.free"], now.last("c"))
                    nc.gpsimd.tensor_tensor(c_xb[:, :], c_x[:, :], gbc[:, :], ALU.add).then_inc(sem["c_xb_done"], 1)
                if s == "c_v1":
                    pool.wait_ge(sem["c_loaded"], now.arrived("c", 16))
                    pool.wait_ge(sem["c_av"], now.group_last("c", 3))
                    nc.gpsimd.tensor_tensor(v1["c"][:, :, 0:HD], c_ctx[:, :].rearrange("p (h i) -> p h i", h=H),
                                            ones[:, 0:HD].unsqueeze(1).broadcast_to([P, H, HD]), ALU.mult).then_inc(sem["c_v1_done"], 1)
                if s == "a_qk":
                    pool.wait_ge(sem["a_qk.free"], now.done("a"))
                    pool.wait_ge(sem["a_tr2.full"], now.last("a"))
                    nc.gpsimd.tensor_tensor(a_qk[:, :], a_c[:, :], a_s[:, :], ALU.add).then_inc(sem["a_rotated"], 1)
                if s == "c_kb":
                    key_blocks(now, "c", "c", "c_qk")
                if s == "d_xb":
                    pool.wait_ge(sem["c_o.free"], now.done("d"))
                    pool.wait_ge(sem["e_o.free"], now.last("d"))
                    nc.gpsimd.tensor_tensor(e_xb[:, :], d_x[:, :], gbo[:, :], ALU.add).then_inc(sem["e_xb_done"], 1)
                if s == "d_kb":
                    key_blocks(now, "e", "d", "d_qk")

            run(pool, ORDERS["pool"], step)

        @block.scalar
        def _(act):
            act.wait_ge(sem["loaded"], 32)
            nc.scalar.activation(tg[:, :], c["g"], ACT.Tanh).then_inc(sem["setup_g"], 1)
            nc.scalar.activation(we_h[:, :], c["we"], ACT.Copy).then_inc(sem["setup_we"], 1)

            def copy(dst, src):
                return nc.scalar.activation(dst, src, ACT.Copy)

            def weigh(now, s):
                act.wait_ge(sem[f"{s}_two_done"], now.done(s))
                nc.scalar.activation(top[s]["e"][:, :], top[s]["mx"][:, 1:2], ACT.Exp, bias=top[s]["n"][:, 0:1]).then_inc(sem[f"{s}_e_done"], 1)

            def exps(now, s, g):
                part = sc[s][:, g % 2]
                if s in BY_DVE:
                    act.wait_ge(sem[f"{s}_s.free"], now.group_done(s, g))
                    nc.scalar.activation(part, part, ACT.Exp).then_inc(sem[f"{s}_exp"], 1)
                else:
                    act.wait_ge(sem[f"{s}_max"], now.group_done(s, g))
                    act.wait_ge(sem[f"{s}_t.full"], now.group_done(s, g - 2))
                    for j in range(GH):
                        ins = nc.scalar.activation(part[:, j], psum(f"{s}_s{g}")[:, j * P:(j + 1) * P], ACT.Exp,
                                                   bias=mx[s][:, GH * g + j:GH * g + j + 1])
                    ins.then_inc(sem[f"{s}_s.free"], 1)

            def keep_probs(now, s, g):
                act.wait_ge(sem[f"{s}_t.full"], now.group_done(s, g))
                act.wait_ge(sem[f"{s}_av"], now.group_done(s, g - 2))
                ins = copy(pt[s][:, g % 2], psum(f"{s}_t{g}").rearrange("p (h q) -> p h q", h=GH))
                ins.then_inc(sem[f"{s}_t.free"], 1)

            def keep_weighted(now, s):
                act.wait_ge(sem[f"{s}_av"], now.group_done(s, 3))
                act.wait_ge(sem[f"{s}_z1.full"], now.last(s))
                copy(z[s][:, :, :], psum(f"{s}_v0").rearrange("p (g q) -> p g q", g=NG)).then_inc(sem[f"{s}_z0.free"], 1)

            def projections(now, step, s, bq, bk, stage):
                act.wait_ge(sem[f"{step}.full"], now.done(stage))
                src = psum(step).rearrange("p (m q) -> p m q", m=2 * KT)
                act.wait_ge(sem[f"{s}_s.full"], now.group_last(stage, 3))
                for m in range(KT):
                    last = nc.scalar.activation(qt[s][:, m], src[:, m], ACT.Identity, bias=bq[:, m:m + 1], scale=SCALE)
                last.then_inc(sem[f"{s}_qt_done"], 1)
                act.wait_ge(sem[f"{s}_kb_done"], now.last(stage))
                for m in range(KT):
                    last = nc.scalar.activation(kt[s][:, m], src[:, KT + m], ACT.Identity, bias=bk[:, m:m + 1])
                last.then_inc(sem[f"{step}.free"], 1)

            def step(now, s):
                if s == "a_tr":
                    act.wait_ge(sem["a_tr.full"], now.done("a"))
                    act.wait_ge(sem["a_v.full"], now.last("a"))
                    copy(a_t[:, :, :], psum(s).rearrange("p (m q) -> p m q", m=2 * KT)).then_inc(sem["a_tr.free"], 1)
                if s == "a_v":
                    act.wait_ge(sem["a_v.full"], now.done("a"))
                    act.wait_ge(sem["a_o.full"], now.last("a"))
                    copy(a_v[:, :], psum(s)[:, 0:D]).then_inc(sem["a_v.free"], 1)
                if s == "a_tr2":
                    act.wait_ge(sem["a_tr2.full"], now.done("a"))
                    act.wait_ge(sem["a_r.full"], now.last("a"))
                    copy(a_qkt[:, :, :], psum(s).rearrange("p (m q) -> p m q", m=2 * KT)).then_inc(sem["a_tr2.free"], 1)
                if s == "b_tr":
                    act.wait_ge(sem["b_tr.full"], now.done("b"))
                    act.wait_ge(sem["b_g.full"], now.last("b"))
                    act.wait_ge(sem["b_lo_done"], now.last("b"))
                    copy(b_t[:, :, :], psum(s)[:, 0:D].rearrange("p (m q) -> p m q", m=KT)).then_inc(sem["b_tr.free"], 1)
                if s == "b_hi":
                    act.wait_ge(sem["b_tr.free"], now.done("b"))
                    act.wait_ge(sem["b_m3.full"], now.last("b"))
                    copy(b_th[:, :, :], b_t[:, :, :]).then_inc(sem["b_hi_done"], 1)
                if s == "b_g":
                    weigh(now, "b")
                if s == "b_w":
                    act.wait_ge(sem["b_w.full"], now.done("b"))
                    act.wait_ge(sem["b_be.full"], now.last("b"))
                    copy(b_wtt[:, :], psum(s)[:, 0:P]).then_inc(sem["b_w.free"], 1)
                if s == "c_tr":
                    act.wait_ge(sem["c_tr.full"], now.done("c"))
                    act.wait_ge(sem["c_qk.full"], now.last("c"))
                    copy(c_t[:, :, :], psum(s).rearrange("p (m q) -> p m q", m=2 * KT)).then_inc(sem["c_tr.free"], 1)
                if s == "c_qk":
                    projections(now, "c_qk", "c", bq1s, c["bk1"], "c")
                if s[0] in "ce" and s[2] == "s":
                    exps(now, s[0], int(s[3]))
                if s[0] in "ce" and s[2] == "t" and s[3].isdigit():
                    keep_probs(now, s[0], int(s[3]))
                if s in ("c_z0", "e_z0"):
                    keep_weighted(now, s[0])
                if s == "c_yt":
                    act.wait_ge(sem["c_yt.full"], now.done("c"))
                    act.wait_ge(sem["c_o.full"], now.last("c"))
                    copy(yt["c"][:, :, :], psum(s)[:, 0:D].rearrange("p (m q) -> p m q", m=KT)).then_inc(sem["c_yt.free"], 1)
                if s == "e_yt":
                    act.wait_ge(sem["e_yt.full"], now.done("e"))
                    act.wait_ge(sem["e_o.full"], now.last("e"))
                    act.wait_ge(sem["e_bv_done"], now.done("e"))
                    for m in range(KT):
                        last = nc.scalar.activation(yt["e"][:, m], psum(s)[:, m * P:(m + 1) * P], ACT.Identity,
                                                    bias=e_bv[:, m:m + 1])
                    last.then_inc(sem["e_yt.free"], 1)
                if s == "d_tr":
                    act.wait_ge(sem["d_tr.full"], now.done("d"))
                    act.wait_ge(sem["d_v.full"], now.last("d"))
                    act.wait_ge(sem["d_h.full"], now.last("d"))
                    for m in range(KT):
                        last = nc.scalar.activation(d_t[:, m], psum(s)[:, m * P:(m + 1) * P], ACT.Copy,
                                                    accum_out=d_pool[:, m:m + 1])
                    last.then_inc(sem["d_tr.free"], 1)
                if s == "d_lg":
                    weigh(now, "d")
                if s in ("d_c0", "d_c1", "d_c2"):
                    j = int(s[3])
                    act.wait_ge(sem["d_weights_done"], now.done("d"))
                    act.wait_ge(sem["d_v.full" if j == 2 else "d_qk.full"], now.last("d"))
                    nc.scalar.activation(d_wx[:, j], wx[:, 0, j * KT * D:(j + 1) * KT * D], ACT.Copy,
                                         scale=top["d"]["w"][:, 0:1]).then_inc(sem[f"d_c{j}_first"], 1)
                if s == "d_qk":
                    act.wait_ge(sem["d_bx"], now.group_done("d", 3))
                    projections(now, "d_qk", "e", d_bx, d_bx[:, KT:2 * KT], "d")
                if s == "d_v":
                    act.wait_ge(sem["d_v.full"], now.done("d"))
                    act.wait_ge(sem["e_av"], now.group_last("d", 3))
                    copy(v1["e"][:, :, 0:HD], psum(s)[:, 0:D].rearrange("p (h i) -> p h i", h=H)).then_inc(sem["d_v.free"], 1)

            run(act, ORDERS["act"], step)

        @block.vector
        def _(dve):
            dve.wait_ge(sem["setup_g"], 1)
            dve.wait_ge(sem["loaded"], 32)
            nc.vector.tensor_scalar(gbc[:, :], c["bc1"], tg[:, 2:3], None, ALU.mult)
            nc.vector.tensor_scalar(gbo[:, :], c["bo"], tg[:, 3:4], None, ALU.mult)
            nc.vector.tensor_scalar(bq1s[:, :], c["bq1"], SCALE, None, ALU.mult)
            nc.vector.memset(ones[:, :], 1.0)
            nc.vector.memset(b_wt[:, :], 0.0)
            for s in "ce":
                nc.vector.memset(v1[s][:, :, HD:2 * HD], 1.0)
            for e in range(E1):
                nc.vector.tensor_scalar(bx[:, e, 0:KT], bx[:, e, 0:KT], SCALE, None, ALU.mult)
            dve.wait_ge(sem["setup_we"], 1)
            nc.vector.tensor_tensor(we_l[:, :], c["we"], we_h[:, :].bitcast(F32), ALU.subtract).then_inc(sem["setup_done"], 1)
            dve.wait_ge(sem["setup_done"], 1)

            def carry_waits(n):
                nc.vector.memset(carrier[:, n:n + 1], 0.0)

            def residual(s, dst, base, gate):
                return nc.vector.scalar_tensor_tensor(dst[:, :], psum(s)[:, 0:D], tg[:, gate:gate + 1], base[:, :], ALU.mult, ALU.add)

            def layer_norm(now, s, part):
                x_of, xn_of = {"a": (a_x, a_xn), "b": (b_x, b_xn), "c": (c_x, c_xn), "d": (d_x, d_xn)}[s]
                if part == "st":
                    if s == "a":
                        dve.wait_ge(sem["a_loaded"], now.arrived("a", 32))
                    else:
                        dve.wait_ge(sem[{"b": "a_o.free", "c": "c_x_done", "d": "c_o.free"}[s]], now.done(s))
                    dve.wait_ge(sem[f"{s}_mv_done"], now.last(s))
                    nc.vector.bn_stats(stats[s][:, :], x_of[:, :]).then_inc(sem[f"{s}_stats_done"], 1)
                if part == "ag":
                    dve.wait_ge(sem[f"{s}_stats_done"], now.done(s))
                    dve.wait_ge(sem[f"{s}_vareps_done"], now.last(s))
                    dve.wait_ge(sem[f"{s}_xn_done"], now.last(s))
                    carry_waits("abcd".index(s))
                    nc.vector.bn_aggr(mv[s][:, :], stats[s][:, :]).then_inc(sem[f"{s}_mv_done"], 1)
                if part == "nm":
                    dve.wait_ge(sem[f"{s}_rstd_done"], now.done(s))
                    dve.wait_ge(sem[f"{s}_tr.full"], now.last(s))
                    nc.vector.tensor_scalar(xn_of[:, :], x_of[:, :], mv[s][:, 0:1], rstd[s][:, 1:2], ALU.subtract,
                                            ALU.mult).then_inc(sem[f"{s}_xn_done"], 1)

            def top_two(now, s, part, logits, bias):
                it = top[s]
                if part == "g0":
                    dve.wait_ge(sem[f"{logits}.full"], now.done(s))
                    dve.wait_ge(sem[f"{s}_ix_done"], now.last(s))
                    nc.vector.tensor_tensor(it["lg"][:, :], psum(logits)[:, 0:8], bias, ALU.add).then_inc(sem[f"{logits}.free"], 1)
                if part == "g1":
                    dve.wait_ge(sem[f"{logits}.free"], now.done(s))
                    dve.wait_ge(sem[f"{s}_e_done"], now.last(s))
                    carry_waits(4 + "bd".index(s))
                    nc.vector.max(it["mx"][:, :], it["lg"][:, :]).then_inc(sem[f"{s}_max_done"], 1)
                if part == "g2":
                    dve.wait_ge(sem[f"{s}_max_done"], now.done(s))
                    dve.wait_ge(sem[f"{s}_if_done"], now.last(s))
                    nc.vector.tensor_scalar(it["n"][:, :], it["mx"][:, 0:1], -1.0, None, ALU.mult).then_inc(sem[f"{s}_two_done"], 1)
                    nc.vector.max_index(it["ix"][:, :], it["mx"][:, :], it["lg"][:, :]).then_inc(sem[f"{s}_ix_done"], 1)
                if part == "g3":
                    dve.wait_ge(sem[f"{s}_ix_done"], now.done(s))
                    dve.wait_ge(sem[f"{s}_placed"], now.last(s))
                    nc.vector.tensor_copy(it["if"][:, :], it["ix"][:, 0:2]).then_inc(sem[f"{s}_if_done"], 1)

            def weights_of(now, s, part, dst):
                it = top[s]
                if part == "w0":
                    dve.wait_ge(sem[f"{s}_e_done"], now.done(s))
                    nc.vector.tensor_scalar(it["s"][:, :], it["e"][:, :], 1.0, None, ALU.add).then_inc(sem[f"{s}_sum_done"], 1)
                if part == "w1":
                    dve.wait_ge(sem[f"{s}_sum_done"], now.done(s))
                    nc.vector.reciprocal(it["r"][:, 0:1], it["s"][:, :]).then_inc(sem[f"{s}_first_done"], 1)
                if part == "w2":
                    dve.wait_ge(sem[f"{s}_first_done"], now.done(s))
                    nc.vector.tensor_tensor(it["r"][:, 1:2], it["r"][:, 0:1], it["e"][:, :], ALU.mult).then_inc(sem[f"{s}_second_done"], 1)
                if part == "w3":
                    dve.wait_ge(sem[f"{s}_second_done"], now.done(s))
                    dve.wait_ge(sem[f"{s}_if_done"], now.done(s))
                    nc.vector.tensor_scalar(it["w1"][:, :], c["iota"], it["if"][:, 0:1], it["r"][:, 0:1], ALU.is_equal, ALU.mult)
                    nc.vector.tensor_scalar(it["w2"][:, :], c["iota"], it["if"][:, 1:2], it["r"][:, 1:2], ALU.is_equal,
                                            ALU.mult).then_inc(sem[f"{s}_placed"], 1)
                if part == "w4":
                    dve.wait_ge(sem[f"{s}_placed"], now.done(s))
                    nc.vector.tensor_tensor(dst, it["w1"][:, :], it["w2"][:, :], ALU.add).then_inc(sem[f"{s}_weights_done"], 1)

            def attention(now, s, part):
                g = int(part[1]) if part[1:].isdigit() else 0
                src = psum(f"{s}_s{g}").rearrange("p (h k) -> p h k", h=GH)
                m = mx[s][:, GH * g:GH * g + GH]
                if part[0] == "m":
                    dve.wait_ge(sem[f"{s}_s.full"], now.group_done(s, g))
                    dve.wait_ge(sem[f"{s}_s.free"], now.group_last(s, g))
                    nc.vector.tensor_reduce(m, src, axis=AX.X, op=ALU.max, negate=s not in BY_DVE).then_inc(sem[f"{s}_max"], 1)
                if part[0] == "s":
                    dve.wait_ge(sem[f"{s}_max"], now.group_done(s, g))
                    dve.wait_ge(sem[f"{s}_t.full"], now.group_done(s, g - 2))
                    nc.vector.tensor_tensor(sc[s][:, g % 2], src, m.unsqueeze(2).broadcast_to([P, GH, P]),
                                            ALU.subtract).then_inc(sem[f"{s}_s.free"], 1)
                heads = psum(f"{s}_z1").rearrange("p (h i) -> p h i", h=H)
                if part == "rz":
                    dve.wait_ge(sem[f"{s}_z1.full"], now.done(s))
                    dve.wait_ge(sem[f"{s}_z1.free"], now.last(s))
                    nc.vector.reciprocal(rz[s][:, :].unsqueeze(2), heads[:, :, HD:HD + 1]).then_inc(sem[f"{s}_rz_done"], 1)
                if part == "y":
                    dve.wait_ge(sem[f"{s}_rz_done"], now.done(s))
                    dve.wait_ge(sem[f"{s}_yt.full"], now.last(s))
                    nc.vector.tensor_tensor(y[s][:, :].rearrange("p (h i) -> p h i", h=H), heads[:, :, 0:HD],
                                            rz[s][:, :].unsqueeze(2).broadcast_to([P, H, HD]), ALU.mult).then_inc(sem[f"{s}_z1.free"], 1)

            def step(now, s):
                if s[2:] in ("st", "ag", "nm"):
                    layer_norm(now, s[0], s[2:])
                if s == "a_qk":
                    dve.wait_ge(sem["a_qk.full"], now.done("a"))
                    dve.wait_ge(sem["a_rotated"], now.last("a"))
                    nc.vector.tensor_tensor(a_c[:, :], psum(s), c["cos"], ALU.mult)
                    pairs, turned, sin = (v.rearrange("p (i two) -> p i two", two=2) for v in (psum(s), a_s[:, :], c["sin"]))
                    nc.vector.tensor_tensor(turned[:, :, 0], pairs[:, :, 1], sin[:, :, 0], ALU.mult)
                    nc.vector.tensor_tensor(turned[:, :, 1], pairs[:, :, 0], sin[:, :, 1], ALU.mult).then_inc(sem["a_qk.free"], 1)
                if s == "a_r":
                    dve.wait_ge(sem["a_r.full"], now.done("a"))
                    dve.wait_ge(sem["a_o.full"], now.last("a"))
                    nc.vector.tensor_tensor(a_ret[:, :], psum(s)[:, 0:P], c["decay"], ALU.mult).then_inc(sem["a_r.free"], 1)
                if s == "a_o":
                    dve.wait_ge(sem["a_o.full"], now.done("a"))
                    dve.wait_ge(sem["c_x_done"], now.last("a"))
                    residual(s, b_x, a_x, 0).then_inc(sem["a_o.free"], 1)
                if s in ("b_g0", "b_g1", "b_g2", "b_g3"):
                    top_two(now, "b", s[2:], "b_g", c["bgate"])
                if s in ("b_w0", "b_w1", "b_w2", "b_w3", "b_w4"):
                    if s == "b_w4":
                        dve.wait_ge(sem["b_w.full"], now.last("b"))
                        dve.wait_ge(sem["b_m3.free"], now.last("b"))
                    weights_of(now, "b", s[2:], b_wt[:, 0:8])
                if s == "b_be":
                    dve.wait_ge(sem["b_be.full"], now.done("b"))
                    dve.wait_ge(sem["c_x_done"], now.last("b"))
                    nc.vector.tensor_copy(b_acc[:, :], psum(s)[:, 0:D]).then_inc(sem["b_be.free"], 1)
                if s[:3] == "b_m":
                    j, i = int(s[3]), "ab".index(s[4])
                    e = 2 * j + i
                    if i:
                        dve.wait_ge(sem["b_half"], now.group_done("b", j))
                    else:
                        dve.wait_ge(sem[f"b_m{j}.full"], now.done("b"))
                        dve.wait_ge(sem[f"b_m{j - 1}.free" if j else "b_be.free"], now.done("b"))
                    nc.vector.scalar_tensor_tensor(b_acc[:, :], psum(s[:4])[:, i * D:(i + 1) * D], b_wt[:, e:e + 1], b_acc[:, :],
                                                   ALU.mult, ALU.add).then_inc(sem[f"b_m{j}.free" if i else "b_half"], 1)
                if s == "b_fin":
                    dve.wait_ge(sem["b_m3.free"], now.done("b"))
                    dve.wait_ge(sem["c_xb_done"], now.last("b"))
                    dve.wait_ge(sem["c_xn_done"], now.last("b"))
                    nc.vector.scalar_tensor_tensor(c_x[:, :], b_acc[:, :], tg[:, 1:2], b_x[:, :], ALU.mult,
                                                   ALU.add).then_inc(sem["c_x_done"], 1)
                if s[0] in "ce" and (s[2:] in ("rz", "y") or s[2] in "ms" and s[3].isdigit()):
                    attention(now, s[0], s[2:])
                if s == "c_o":
                    dve.wait_ge(sem["c_o.full"], now.done("c"))
                    dve.wait_ge(sem["c_xb_done"], now.done("c"))
                    dve.wait_ge(sem["e_xb_done"], now.last("c"))
                    dve.wait_ge(sem["d_xn_done"], now.last("c"))
                    residual(s, d_x, c_xb, 2).then_inc(sem["c_o.free"], 1)
                if s == "e_o":
                    dve.wait_ge(sem["e_o.full"], now.done("e"))
                    dve.wait_ge(sem["e_xb_done"], now.done("e"))
                    dve.wait_ge(sem["stored"], now.count(16, -16 * LAG["e"]))
                    residual(s, e_out, e_xb, 3).then_inc(sem["e_o.free"], 1)
                if s == "d_h":
                    dve.wait_ge(sem["d_h.full"], now.done("d"))
                    dve.wait_ge(sem["d_hb_done"], now.last("d"))
                    nc.vector.tensor_scalar(d_h[:, :], psum(s)[:, 0:1], 1.0 / P, c["bh"], ALU.mult, ALU.add).then_inc(sem["d_h.free"], 1)
                if s == "d_hb":
                    dve.wait_ge(sem["d_h.free"], now.done("d"))
                    dve.wait_ge(sem["d_lg.full"], now.last("d"))
                    nc.vector.tensor_scalar(d_hb[:, :], ones[:, :], d_h[:, 0:1], 0.0, ALU.mult, ALU.max).then_inc(sem["d_hb_done"], 1)
                if s in ("d_g0", "d_g1", "d_g2", "d_g3"):
                    top_two(now, "d", s[2:], "d_lg", c["bl"])
                if s in ("d_w0", "d_w1", "d_w2", "d_w3", "d_w4"):
                    if s == "d_w4":
                        dve.wait_ge(sem["d_c2_first"], now.last("d"))
                        dve.wait_ge(sem["d_c2_done"], now.last("d"))
                        dve.wait_ge(sem["d_bx"], now.group_last("d", 3))
                    weights_of(now, "d", s[2:], top["d"]["w"][:, :])
                if s in ("d_b0", "d_b1", "d_b2", "d_b3"):
                    e, w = int(s[3]), top["d"]["w"]
                    if e == 0:
                        dve.wait_ge(sem["d_weights_done"], now.done("d"))
                        dve.wait_ge(sem["d_qk.free"], now.last("d"))
                        dve.wait_ge(sem["e_bv_done"], now.last("d"))
                        nc.vector.tensor_scalar(d_bx[:, :], bx[:, 0], w[:, 0:1], None, ALU.mult).then_inc(sem["d_bx"], 1)
                    else:
                        dve.wait_ge(sem["d_bx"], now.group_done("d", e - 1))
                        nc.vector.scalar_tensor_tensor(d_bx[:, :], bx[:, e], w[:, e:e + 1], d_bx[:, :], ALU.mult,
                                                       ALU.add).then_inc(sem["d_bx"], 1)
                if s[:3] == "d_c":
                    j, e = int(s[3]), 1 + "abc".index(s[4])
                    w, n = top["d"]["w"], KT * D
                    if e == 1:
                        dve.wait_ge(sem[f"d_c{j}_first"], now.done("d"))
                    else:
                        dve.wait_ge(sem[f"d_c{j}_{e - 1}"], now.done("d"))
                    nc.vector.scalar_tensor_tensor(d_wx[:, j], wx[:, e, j * n:(j + 1) * n], w[:, e:e + 1], d_wx[:, j],
                                                   ALU.mult, ALU.add).then_inc(sem[f"d_c{j}_done" if e == E1 - 1 else f"d_c{j}_{e}"], 1)
                if s == "d_bv":
                    dve.wait_ge(sem["d_bx"], now.group_done("d", 3))
                    dve.wait_ge(sem["e_yt.free"], now.last("d"))
                    nc.vector.tensor_copy(e_bv[:, :], d_bx[:, 2 * KT:3 * KT]).then_inc(sem["e_bv_done"], 1)

            run(dve, ORDERS["dve"], step)

        @block.tensor
        def _(pe):
            pe.wait_ge(sem["loaded"], 32)
            pe.wait_ge(sem["setup_done"], 1)

            def mm(dst, lhs, rhs, k=0, last=0):
                return nc.tensor.matmul(dst, lhs, rhs, start=k == 0, stop=k == last)

            def transposes(s, tiles):
                out = psum(s).rearrange("p (m q) -> p m q", m=2 * KT)
                for m, tile in enumerate(tiles):
                    ins = nc.tensor.transpose(out[:, m], tile, ident)
                return ins

            def halves(tile):
                return [tile[:, m * P:(m + 1) * P] for m in range(KT)]

            def by_tokens(s, lhs, rhs, n, at=0):
                for k in range(KT):
                    ins = mm(psum(s)[:, at:at + n], lhs[:, k], rhs[:, k], k, KT - 1)
                return ins

            def by_channels(s, at, w, rhs):
                for m in range(KT):
                    for k in range(KT):
                        ins = mm(psum(s)[:, (at + m) * P:(at + m + 1) * P], w[:, k, m * P:(m + 1) * P], rhs[:, k], k, KT - 1)
                return ins

            def attention(now, s, step):
                g = int(step[3])
                if step[2] == "s":
                    made_by = "d" if s == "e" else "c"
                    if g == 0:
                        pe.wait_ge(sem[f"{s}_qt_done"], now.done(s))
                        pe.wait_ge(sem[f"{s}_kb_done"], now.done(s))
                    m, at = g * GH // E0, g * GH % E0
                    mm(psum(step).rearrange("p (h k) -> p h k", h=GH), qt[s][:, m], kb[s][:, m, at:at + GH]).then_inc(sem[f"{s}_s.full"], 1)
                elif step[2] == "t":
                    pe.wait_ge(sem[f"{s}_exp" if s in BY_DVE else f"{s}_s.free"], now.group_done(s, g))
                    transposes(step, [sc[s][:, g % 2, j] for j in range(GH)]).then_inc(sem[f"{s}_t.full"], 1)
                else:
                    pe.wait_ge(sem[f"{s}_t.free"], now.group_done(s, g))
                    if g == 0:
                        pe.wait_ge(sem[f"{s}_v1_done" if s == "c" else "d_v.free"], now.done(s))
                    for j in range(GH):
                        ins = nc.tensor.matmul(psum(step)[32 * j:32 * j + 32, g * P:(g + 1) * P], v1[s][:, GH * g + j],
                                               pt[s][:, g % 2, j], start=True, stop=True, tile_position=(0, 32 * j))
                    ins.then_inc(sem[f"{s}_av"], 1)

            def step(now, s):
                if TAKES[s]:
                    pe.wait_ge(sem[now.reader(s)], now.released(s))
                heads = s in GROUPED
                full = sem[f"{s}.full"] if TAKES[s] and not heads else None
                if s == "a_tr":
                    pe.wait_ge(sem["a_xn_done"], now.done("a"))
                    transposes(s, halves(a_xn) + halves(a_ctx)).then_inc(full, 1)
                if s == "a_qk":
                    pe.wait_ge(sem["a_tr.free"], now.done("a"))
                    by_tokens(s, a_t[:, 0:KT], wq0, D)
                    by_tokens(s, a_t[:, KT:2 * KT], wk0, D, at=D).then_inc(full, 1)
                if s == "a_v":
                    by_tokens(s, a_t[:, KT:2 * KT], wv0, D).then_inc(full, 1)
                if s == "a_tr2":
                    pe.wait_ge(sem["a_rotated"], now.done("a"))
                    transposes(s, halves(a_qk[:, 0:D]) + halves(a_qk[:, D:2 * D])).then_inc(full, 1)
                if s == "a_r":
                    pe.wait_ge(sem["a_tr2.free"], now.done("a"))
                    for k in range(KT):
                        ins = mm(psum(s)[:, 0:P], a_qkt[:, KT + k], a_qkt[:, k], k, KT - 1)
                    ins.then_inc(full, 1)
                if s == "a_o":
                    pe.wait_ge(sem["a_r.free"], now.done("a"))
                    pe.wait_ge(sem["a_v.free"], now.done("a"))
                    mm(psum(s)[:, 0:D], a_ret[:, :], a_v[:, :]).then_inc(full, 1)
                if s == "b_tr":
                    pe.wait_ge(sem["b_xn_done"], now.done("b"))
                    transposes(s, halves(b_xn)).then_inc(full, 1)
                if s == "b_g":
                    pe.wait_ge(sem["b_tr.free"], now.done("b"))
                    by_tokens(s, b_t, wgate, P).then_inc(full, 1)
                if s == "b_w":
                    pe.wait_ge(sem["b_weights_done"], now.done("b"))
                    nc.tensor.transpose(psum(s)[:, 0:P], b_wt[:, :], ident).then_inc(full, 1)
                if s == "b_be":
                    pe.wait_ge(sem["b_w.free"], now.done("b"))
                    mm(psum(s)[:, 0:D], b_wtt[:, :], c["be"]).then_inc(full, 1)
                if s in ("b_m0", "b_m1", "b_m2", "b_m3"):
                    j = int(s[3])
                    experts = slice(2 * j * D, 2 * (j + 1) * D)
                    if j == 0:
                        pe.wait_ge(sem["b_lo_done"], now.done("b"))
                    passes = [(x, w, k) for x, w in ((b_th, we_hi), (b_tl, we_hi), (b_th, we_lo)) for k in range(KT)]
                    for n, (x, w, k) in enumerate(passes):
                        ins = mm(psum(s), x[:, k], w[:, k, experts], n, len(passes) - 1)
                    ins.then_inc(full, 1)
                if s == "c_tr":
                    pe.wait_ge(sem["c_xn_done"], now.done("c"))
                    pe.wait_ge(sem["c_loaded"], now.arrived("c", 16))
                    transposes(s, halves(c_xn) + halves(c_ctx)).then_inc(full, 1)
                if s == "c_qk":
                    pe.wait_ge(sem["c_tr.free"], now.done("c"))
                    by_channels(s, 0, wq1, c_t[:, 0:KT])
                    by_channels(s, KT, wk1, c_t[:, KT:2 * KT]).then_inc(full, 1)
                if s == "d_tr":
                    pe.wait_ge(sem["d_xn_done"], now.done("d"))
                    transposes(s, halves(d_xn)).then_inc(full, 1)
                if s == "d_h":
                    pe.wait_ge(sem["d_tr.free"], now.done("d"))
                    for k in range(KT):
                        ins = mm(psum(s)[:, 0:1], wh[:, k], d_pool[:, k:k + 1], k, KT - 1)
                    ins.then_inc(full, 1)
                if s == "d_lg":
                    pe.wait_ge(sem["d_hb_done"], now.done("d"))
                    mm(psum(s)[:, 0:8], d_hb[:, :], c["wl"]).then_inc(full, 1)
                if s == "d_qk":
                    pe.wait_ge(sem["d_c0_done"], now.done("d"))
                    by_channels(s, 0, d_wx[:, 0].rearrange("p (k n) -> p k n", k=KT), d_t)
                    pe.wait_ge(sem["d_c1_done"], now.done("d"))
                    by_channels(s, KT, d_wx[:, 1].rearrange("p (k n) -> p k n", k=KT), d_t).then_inc(full, 1)
                if s == "d_v":
                    pe.wait_ge(sem["d_c2_done"], now.done("d"))
                    by_tokens(s, d_t, d_wx[:, 2].rearrange("p (k n) -> p k n", k=KT), D).then_inc(full, 1)
                if heads:
                    attention(now, s[0], s)
                if s in ("c_z1", "e_z1"):
                    pe.wait_ge(sem[f"{s[0]}_z0.free"], now.done(s[0]))
                    transposes(s, [z[s[0]][:, g] for g in range(NG)]).then_inc(full, 1)
                if s in ("c_yt", "e_yt"):
                    pe.wait_ge(sem[f"{s[0]}_z1.free"], now.done(s[0]))
                    transposes(s, halves(y[s[0]])).then_inc(full, 1)
                if s in ("c_o", "e_o"):
                    pe.wait_ge(sem[f"{s[0]}_yt.free"], now.done(s[0]))
                    by_tokens(s, yt[s[0]], wc1 if s[0] == "c" else wo, D).then_inc(full, 1)

            run(pe, ORDERS["pe"], step)


def shape_tables():
    f = np.float32
    base = (np.arange(0, D, 2, dtype=f) + f(0.4 * D)) / f(1.4 * D)
    pos = np.arange(P, dtype=f)
    scale = base[None, :] ** (pos[:, None] / f(512.0))
    freqs = f(1.0) / f(10000.0) ** (np.arange(D // 2, dtype=f) / f(D // 2))
    angle = pos[:, None] * freqs[None, :]
    sign = np.tile(np.array([-1.0, 1.0], f), D // 2)

    def twice(a):
        return np.repeat(a, 2, axis=1).astype(f)

    u, v = np.arange(P)[None, :], np.arange(P)[:, None]
    decay = np.where(u >= v, f(GAMMA) ** np.maximum(u - v, 0).astype(f), f(0))
    heads = (np.arange(P)[:, None] // HD == np.arange(E0)[None, :])
    rows = {
        "cos": np.concatenate([twice(np.cos(angle) * s) for s in (scale, f(1) / scale)], axis=1),
        "sin": np.concatenate([twice(np.sin(angle) * s) * sign for s in (scale, f(1) / scale)], axis=1),
        "decay": decay, "ident": np.eye(P), "heads": heads, "iota": np.tile(np.arange(E0), (P, 1)),
        "eps": np.tile(np.array([EPS, -0.5]), (P, 1)),
    }
    return np.concatenate([rows[name].astype(f).reshape(P, n) for name, n in TABLES], axis=1)


def laid_out(i):
    def tiles(w):
        return w.reshape(KT, P, -1).transpose(1, 0, 2).reshape(P, -1)

    def everywhere(v, n=None):
        v = v.reshape(1, -1)
        return np.broadcast_to(v, (P, v.shape[1]))

    def columns(v):
        return v.reshape(KT, P).T

    def wider(w, rows, cols, fill=0.0):
        out = np.full((rows, cols), fill, np.float32)
        out[:w.shape[0], :w.shape[1]] = w
        return out

    mixed = np.stack([i["L1_ffn_Wq"], i["L1_ffn_Wk"], i["L1_ffn_Wv"]], axis=1).reshape(E1, 3, KT, P, D)
    mixed_b = np.stack([i["L1_ffn_bq"], i["L1_ffn_bk"], i["L1_ffn_bv"]], axis=1).reshape(E1, 3, KT, P)
    gates = np.stack([i["g_xattn"][0], i["g_ffn"][0], i["g_xattn"][1], i["g_ffn"][1]])
    parts = {
        "wq0": tiles(i["L0_xattn_Wq"].T),
        "wk0": tiles(i["L0_xattn_Wk"].T), "wv0": tiles(i["L0_xattn_Wv"].T),
        "we": tiles(i["L0_ffn_We"].transpose(2, 0, 1).reshape(D, E0 * D)),
        "be": wider(i["L0_ffn_be"], P, D), "wgate": tiles(wider(i["L0_ffn_Wg"], D, P)), "bgate": everywhere(i["L0_ffn_bg"]),
        "wq1": tiles(i["L1_xattn_Wq"].T), "wk1": tiles(i["L1_xattn_Wk"].T), "bq1": columns(i["L1_xattn_bq"]),
        "bk1": columns(i["L1_xattn_bk"]), "wc1": tiles(i["L1_xattn_Wc"].T), "bc1": everywhere(i["L1_xattn_bc"]),
        "wx": mixed.transpose(3, 0, 1, 2, 4).reshape(P, -1), "bx": mixed_b.transpose(3, 0, 1, 2).reshape(P, -1),
        "wh": tiles(i["L1_ffn_Wg1"]), "bh": i["L1_ffn_bg1"].reshape(P, 1), "wl": wider(i["L1_ffn_Wg2"], P, E0),
        "bl": everywhere(wider(i["L1_ffn_bg2"].reshape(1, E1), 1, E0, NEG)), "wo": tiles(i["L1_ffn_Wo"]),
        "bo": everywhere(i["L1_ffn_bo"]), "g": everywhere(gates),
    }
    return np.ascontiguousarray(np.concatenate([parts[name].reshape(P, n) for name, n in WEIGHTS], axis=1))


def kernel(**inputs):
    import concourse.bacc as bacc
    from concourse.bass_utils import run_bass_kernel_spmd

    i = {name: np.asarray(a) for name, a in inputs.items()}
    arrays = {"x": np.ascontiguousarray(i["x"]), "ctx": np.ascontiguousarray(i["ctx_1024"]), "weights": laid_out(i),
              "tables": shape_tables()}
    nc = bacc.Bacc("TRN2", target_bir_lowering=False, num_devices=1)
    aps = [nc.dram_tensor(name, a.shape, F32, kind="ExternalInput").ap() for name, a in arrays.items()]
    out = nc.dram_tensor("out", (NB, P, D), F32, kind="ExternalOutput").ap()
    build(nc, *aps, out)
    result = run_bass_kernel_spmd(nc, [arrays], core_ids=[0])
    return result.results[0]["out"]
```

```python
import numpy as np
import concourse.bass as bass
from concourse import mybir
from contextlib import ExitStack

F32 = mybir.dt.float32
F32R = mybir.dt.float32r
U32 = mybir.dt.uint32
ALU = mybir.AluOpType
ACT = mybir.ActivationFunctionType
AX = mybir.AxisListType

NB = 32
P = 128
D = 256
KT = D // P
H = 16
HD = D // H
NG = 4
GH = H // NG
E0 = 8
E1 = 4
GAMMA = 0.96875
EPS = 1e-5
SCALE = 1.0 / float(np.sqrt(HD))
NEG = -3.0e38

LAG = {"a": 0, "b": 1, "c": 2, "d": 3, "e": 4}
DEPTH = max(LAG.values())
NORM_WITH = {"a": "a", "b": "a", "c": "b", "d": "d"}
UNROLL = 3
RING = UNROLL

ORDERS = {
    "pe": """
        b_tr e_s0 b_g c_tr e_s1 c_qk d_tr e_s2 a_tr d_h e_t0 e_s3 b_w d_lg c_s0 a_qk b_be c_s1 e_t1 b_m0 b_m1
        c_s2 e_v0 a_tr2 c_t0 b_m2 c_s3 e_t2 a_v a_r b_m3 c_t1 a_o e_v1 e_t3 d_qk e_v2 e_v3 c_t2 c_v0 c_v1 c_t3
        e_o c_v2 c_v3 d_v c_o
    """.split(),
    "dve": """
        d_st e_m0 d_ag b_g0 b_g1 a_st a_ag b_g2 d_nm e_r0 b_w0 a_nm b_w1 b_w2 e_m1 b_g3 b_w3 d_h d_hb b_w4 e_m2
        d_g0 e_r1 d_g1 e_m3 d_g2 c_m0 d_w0 e_r2 d_g3 d_w1 a_q0 a_q1 d_w2 a_q2 b_be d_w3 c_m1 d_w4 b_m0a c_r0
        d_b0 b_m0b d_c1a b_m1a d_c0a d_b1 e_r3 b_m1b c_m2 b_m2a c_r1 d_c1b b_m2b d_c0b c_m3 a_r d_b2 d_c0c d_c1c
        c_r2 d_b3 d_c2a c_r3 b_m3a a_o b_m3b d_c2b b_st d_c2c b_ag b_fin e_o c_st b_nm c_ag c_o d_bv c_nm
    """.split(),
    "act": """
        b_tr b_hi c_tr e_s0 b_g c_k d_tr c_q a_tr e_s1 e_s2 d_lg b_w c_s0 e_t0 e_s3 d_c1 d_c0 c_s1 a_tr2 e_t1
        c_t0 c_s2 a_v e_t2 d_c2 c_s3 e_t3 c_t1 d_k e_yt c_t2 c_t3 d_q c_yt d_v
    """.split(),
    "pool": """
        d_ve d_rs a_ve a_rs e_p0 c_kb0 c_vp c_xb b_lo e_p1 c_kb1 a_qk c_p0 e_p2 e_p3 c_p1 c_p2 c_p3 d_kb0 b_ve
        b_rs d_xb c_ve c_rs d_kb1
    """.split(),
    "sp": """
        a_in e_out
    """.split(),
}
BANK = {
    "a_o": "bank4", "a_qk": "bank5", "a_r": "bank3", "a_tr": "bank3", "a_tr2": "bank1", "a_v": "bank5",
    "b_be": "bank1", "b_g": "bank6", "b_m0": "bank7", "b_m1": "bank5", "b_m2": "bank7", "b_m3": "bank1",
    "b_tr": "bank1", "b_w": "bank7", "c_o": "bank5", "c_qk": "bank6", "c_s0": "bank3", "c_s1": "bank0",
    "c_s2": "bank4", "c_s3": "bank0", "c_t0": "bank3", "c_t1": "bank5", "c_t2": "bank5", "c_t3": "bank1",
    "c_tr": "bank7", "c_v": "bank4", "d_h": "bank5", "d_lg": "bank5", "d_qk": "bank7", "d_tr": "bank7",
    "d_v": "bank0", "e_o": "bank2", "e_s0": "bank2", "e_s1": "bank1", "e_s2": "bank0", "e_s3": "bank4",
    "e_t0": "bank2", "e_t1": "bank6", "e_t2": "bank6", "e_t3": "bank3", "e_v": "bank2",
}
TAKES = {s: (BANK["c_v"] if s[0] == "c" else BANK["e_v"]) if s[2:] == "v0" else BANK.get(s) for s in ORDERS["pe"]}


GROUPED = {s for s in ORDERS["pe"] if s[0] in "ce" and s[2] in "stv" and s[3].isdigit()}


def lag(step):
    return LAG[NORM_WITH[step[0]] if step[2:] in ("st", "ag", "nm", "ve", "rs") else step[0]]


def before(bank, step, t):
    users = [s for s in ORDERS["pe"] if TAKES[s] == bank]
    at = users.index(step)
    for back in range(1, len(users) * (DEPTH + 2) + 1):
        user, turns = users[(at - back) % len(users)], (at - back) // len(users)
        batch = t - LAG[user[0]] + turns
        if not isinstance(t, int) or 0 <= batch < NB:
            return user, batch
    return None


WEIGHTS = {
    "a": [
        ("g", 4), ("bgate", E0), ("bq1", KT), ("bk1", KT), ("bc1", D), ("bx", E1 * 3 * KT), ("bh", 1), ("wl", E0), ("bl", E0),
        ("bo", D), ("wq0", KT * D), ("wk0", KT * D), ("wv0", KT * D),
    ],
    "b": [("wgate", KT * E0), ("we", KT * E0 * D), ("be", D)],
    "c": [("wq1", KT * D), ("wk1", KT * D), ("wc1", KT * D)],
    "d": [("wh", KT * P), ("wx", E1 * 3 * KT * D), ("wo", KT * D)],
}
PACKED = [part for parts in WEIGHTS.values() for part in parts]
TABLES = [
    ("cos", 2 * D), ("sin", 2 * D), ("decay", P), ("ident", P), ("heads", E0), ("iota", E0), ("eps", 2),
]


def build(nc, x, ctx_in, weights, tables, out):
    with ExitStack() as stack:
        def sb(name, *shape, dt=F32):
            return stack.enter_context(nc.sbuf_tensor(name, [P, *shape], dt))

        def ring(name, *shape):
            return [sb(f"{name}{n}", *shape) for n in range(RING)]

        wsum, tsum = sum(n for _, n in PACKED), sum(n for _, n in TABLES)
        w_sb, t_sb = sb("w_sb", wsum), sb("t_sb", tsum)
        c = {}
        for tile, parts in ((w_sb, PACKED), (t_sb, TABLES)):
            at = 0
            for name, n in parts:
                c[name] = tile[:, at:at + n]
                at += n
        wq0 = c["wq0"].rearrange("p (k n) -> p k n", k=KT)
        wk0 = c["wk0"].rearrange("p (k n) -> p k n", k=KT)
        wv0 = c["wv0"].rearrange("p (k n) -> p k n", k=KT)
        we_h, we_l = sb("we_h", KT * E0 * D, dt=F32R), sb("we_l", KT * E0 * D, dt=F32R)
        we_hi, we_lo = (w[:, :].rearrange("p (k n) -> p k n", k=KT) for w in (we_h, we_l))
        wgate = c["wgate"].rearrange("p (k n) -> p k n", k=KT)
        wq1 = c["wq1"].rearrange("p (k n) -> p k n", k=KT)
        wk1 = c["wk1"].rearrange("p (k n) -> p k n", k=KT)
        wc1 = c["wc1"].rearrange("p (k n) -> p k n", k=KT)
        wx = c["wx"].rearrange("p (e n) -> p e n", e=E1)
        bx = c["bx"].rearrange("p (e n) -> p e n", e=E1)
        wh = c["wh"].rearrange("p (k n) -> p k n", k=KT)
        wo = c["wo"].rearrange("p (k n) -> p k n", k=KT)
        ident = c["ident"]

        tg = sb("tg", 4)
        gbc, gbo = sb("gbc", D), sb("gbo", D)
        bq1s = sb("bq1s", KT)
        ones, carrier = sb("ones", P), sb("carrier", 6)

        a_x, b_x, c_x, d_x, ctx = (ring(n, D) for n in ("a_x", "b_x", "c_x", "d_x", "ctx"))
        a_t = ring("a_t", 2 * KT, P)
        a_xn = sb("a_xn", D)
        a_qk, a_qkt = sb("a_qk", 2 * D), sb("a_qkt", 2 * KT, P)
        a_c, a_s = sb("a_c", 2 * D), sb("a_s", 2 * D)
        a_v, a_ret = sb("a_v", D), sb("a_ret", P)
        b_xn, b_t = sb("b_xn", D), sb("b_t", KT, P)
        b_th, b_tl = sb("b_th", KT, P, dt=F32R), sb("b_tl", KT, P, dt=F32R)
        b_wt, b_wtt, b_acc = sb("b_wt", P), sb("b_wtt", P), sb("b_acc", D)
        c_xb, c_xn, c_t = sb("c_xb", D), sb("c_xn", D), sb("c_t", KT, P)
        d_xn, d_t, d_pool = sb("d_xn", D), sb("d_t", KT, P), sb("d_pool", KT)
        d_h, d_hb = sb("d_h", 1), sb("d_hb", P)
        d_wx, d_bx = sb("d_wx", 3, KT * D), sb("d_bx", 3 * KT)
        e_xb, e_out, e_bv = sb("e_xb", D), sb("e_out", D), sb("e_bv", KT)
        stats = {s: sb(f"{s}_stats", 6) for s in "abcd"}
        mv = {s: sb(f"{s}_mv", 2) for s in "abcd"}
        rstd = {s: sb(f"{s}_rstd", 2) for s in "abcd"}
        top = {s: {"lg": sb(f"{s}_lg", 8), "mx": sb(f"{s}_mx", 8), "ix": sb(f"{s}_ix", 8, dt=U32), "if": sb(f"{s}_if", 2),
                   "n": sb(f"{s}_n", 1), "e": sb(f"{s}_e", 1), "s": sb(f"{s}_s", 1), "r": sb(f"{s}_r", 2),
                   "w1": sb(f"{s}_w1", 8), "w2": sb(f"{s}_w2", 8), "w": sb(f"{s}_wts", 8)} for s in "bd"}
        qt = {s: sb(f"{s}_qt", KT, P) for s in "ce"}
        kt = {s: sb(f"{s}_kt", KT, P) for s in "ce"}
        kb = {s: sb(f"{s}_kb", KT, E0, P) for s in "ce"}
        vp = {s: sb(f"{s}_vp", H // 2, 3 * HD) for s in "ce"}
        mx = {s: sb(f"{s}_smx", H) for s in "ce"}
        sc = {s: sb(f"{s}_sc", 2, GH, P) for s in "ce"}
        pt = {s: sb(f"{s}_pt", 2, GH, P) for s in "ce"}
        sums, rz = ({s: sb(f"{s}_{n}", H) for s in "ce"} for n in ("sums", "rz"))
        yt = {s: sb(f"{s}_yt", KT, P) for s in "ce"}

        bank = {n: stack.enter_context(nc.psum_tensor(n, [P, 512], F32)) for n in (f"bank{k}" for k in range(8))}

        def psum(step):
            return bank[BANK[step[:3] if step[2] == "v" and step[0] in "ce" else step]][:, :]

        def pairs_of_heads(s):
            return vp[s][:, :, :].rearrange("p h (e i) -> p h e i", i=HD)[:, :, 0:3:2]

        class Semaphores(dict):

            def __missing__(self, event):
                self[event] = stack.enter_context(nc.semaphore(event.replace(".", "_")))
                return self[event]

        sem = Semaphores()
        loaded = [sem[f"loaded_{n}"] for n in range(RING)]

        block = stack.enter_context(nc.Block())

        class Turn:

            def __init__(self, eng, t, ahead):
                self.eng, self.t, self.ahead, self.counts = eng, t, ahead, {}

            def count(self, per, n):
                if isinstance(self.t, int):
                    return max(self.t * per + n, 0)
                if (per, n) not in self.counts:
                    self.counts[per, n] = self.eng.snap(self.t * (UNROLL * per) + (self.ahead * per + n))
                return self.counts[per, n]

            def done(self, stage):
                return self.count(1, 1 - LAG[stage])

            def last(self, stage):
                return self.count(1, -LAG[stage])

            def group_done(self, stage, g):
                return self.count(NG, -NG * LAG[stage] + g + 1)

            def group_last(self, stage, g):
                return self.count(NG, -NG * LAG[stage] + g + 1 - NG)

            def half_done(self, stage, m):
                return self.count(KT, -KT * LAG[stage] + m + 1)

            def half_last(self, stage, m):
                return self.count(KT, -KT * LAG[stage] + m + 1 - KT)

            def slot(self, stage, ring):
                return ring[((self.t if isinstance(self.t, int) else self.ahead) - LAG[stage]) % RING]

            def slot_free(self, stage):
                return self.count(1, 1 - LAG[stage] - RING)

            def arrived(self, stage, each):
                if isinstance(self.t, int):
                    return ((self.t - LAG[stage]) // RING + 1) * each
                return self.eng.snap(self.t * each + ((self.ahead - LAG[stage]) // RING + 1) * each)

            def user(self, step):
                if isinstance(self.t, int):
                    return before(TAKES[step], step, self.t) or (step, -1)
                users = [s for s in ORDERS["pe"] if TAKES[s] == TAKES[step]]
                at = users.index(step)
                return users[at - 1], -LAG[users[at - 1][0]] - (at == 0)

            def reader(self, step):
                user, _ = self.user(step)
                if user[2:] == "v0":
                    return user[0] + "_yt.free"
                return user[:3] + ".free" if user in GROUPED else user + ".free"

            def released(self, step):
                user, batch = self.user(step)
                per, n = (NG, int(user[3]) + 1) if user in GROUPED and user[2] != "v" else (1, 1)
                if isinstance(self.t, int):
                    return max(batch * per + n, 0)
                return self.count(per, batch * per + n)

        def run(eng, order, step_fn, begin=None):
            def turn(t, steps, ahead=0):
                now = Turn(eng, t, ahead)
                for s in steps:
                    step_fn(now, s)
            for t in range(DEPTH + 1):
                if begin:
                    begin(t)
                turn(t, [s for s in order if t >= lag(s)])
            with eng.Fori(0, (NB - DEPTH - 1) // UNROLL) as n:
                for ahead in range(UNROLL):
                    turn(n, order, DEPTH + 1 + ahead)
            for t in range(NB, NB + DEPTH):
                turn(t, [s for s in order if t - lag(s) < NB])

        x_rows = x.rearrange("b p d -> (b p) d")
        ctx_rows = ctx_in.rearrange("b p d -> (b p) d")
        out_rows = out.rearrange("b p d -> (b p) d")

        @block.sync
        def _(sp):
            ends = np.cumsum([sum(n for _, n in parts) for parts in WEIGHTS.values()]).tolist()
            sp.dma_start(t_sb[:, :], tables).then_inc(sem["loaded"], 16)
            sp.dma_start(w_sb[:, 0:ends[0]], weights[:, 0:ends[0]]).then_inc(sem["loaded"], 16)

            def begin(t):
                if t == 1:
                    for s, at, end in zip("bcd", ends, ends[1:]):
                        sp.dma_start(w_sb[:, at:end], weights[:, at:end]).then_inc(sem[f"loaded_{s}"], 16)

            def rows(now, lag):
                if isinstance(now.t, int):
                    return bass.ds((now.t - lag) * P, P)
                return bass.ds(now.t * (UNROLL * P) + (now.ahead - lag) * P, P)

            def step(now, s):
                if s == "a_in":
                    sp.wait_ge(sem["a_o.free"], now.slot_free("a"))
                    sp.wait_ge(sem["c_vp_done"], now.slot_free("a"))
                    sp.dma_start(now.slot("a", a_x)[:, :], x_rows[rows(now, 0), :]).then_inc(now.slot("a", loaded), 16)
                    sp.dma_start(now.slot("a", ctx)[:, :], ctx_rows[rows(now, 0), :]).then_inc(now.slot("a", loaded), 16)
                if s == "e_out":
                    sp.wait_ge(sem["e_o.free"], now.done("e"))
                    sp.dma_start(out_rows[rows(now, LAG["e"]), :], e_out[:, :]).then_inc(sem["stored"], 16)

            run(sp, ORDERS["sp"], step, begin)
            sp.wait_ge(sem["stored"], 16 * NB)

        @block.gpsimd
        def _(pool):
            pool.wait_ge(sem["setup_done"], 1)

            def key_blocks(now, s, made_by, m):
                pool.wait_ge(sem[f"{s}_kt_done"], now.done(made_by))
                pool.wait_ge(sem[f"{s}_s.full"], now.group_last(made_by, NG // KT * (m + 1) - 1))
                nc.gpsimd.tensor_tensor(
                    kb[s][:, m], kt[s][:, m].unsqueeze(1).broadcast_to([P, E0, P]),
                    c["heads"].unsqueeze(2).broadcast_to([P, E0, P]), ALU.mult).then_inc(sem[f"{s}_kb_done"], 1)

            def step(now, s):
                if s[2:] == "ve":
                    pool.wait_ge(sem[f"{s[0]}_mv_done"], now.done(NORM_WITH[s[0]]))
                    nc.gpsimd.tensor_tensor(rstd[s[0]][:, 0:1], mv[s[0]][:, 1:2], c["eps"][:, 0:1], ALU.add).then_inc(sem[f"{s[0]}_vareps_done"], 1)
                if s[2:] == "rs":
                    pool.wait_ge(sem[f"{s[0]}_vareps_done"], now.done(NORM_WITH[s[0]]))
                    pool.wait_ge(sem[f"{s[0]}_xn_done"], now.last(NORM_WITH[s[0]]))
                    nc.gpsimd.tensor_tensor(rstd[s[0]][:, 1:2], rstd[s[0]][:, 0:1], c["eps"][:, 1:2], ALU.pow).then_inc(sem[f"{s[0]}_rstd_done"], 1)
                if s == "b_lo":
                    pool.wait_ge(sem["b_hi_done"], now.done("b"))
                    pool.wait_ge(sem["b_m3.full"], now.last("b"))
                    nc.gpsimd.tensor_tensor(b_tl[:, :, :], b_t[:, :, :], b_th[:, :, :].bitcast(F32), ALU.subtract).then_inc(sem["b_lo_done"], 1)
                if s == "c_xb":
                    pool.wait_ge(sem["c_x_done"], now.done("c"))
                    pool.wait_ge(sem["c_o.free"], now.last("c"))
                    nc.gpsimd.tensor_tensor(c_xb[:, :], now.slot("c", c_x)[:, :], gbc[:, :], ALU.add).then_inc(sem["c_xb_done"], 1)
                if s == "c_vp":
                    pool.wait_ge(now.slot("c", loaded), now.arrived("c", 32))
                    pool.wait_ge(sem["c_av"], now.group_last("c", 3))
                    nc.gpsimd.tensor_tensor(
                        pairs_of_heads("c"), now.slot("c", ctx)[:, :].rearrange("p (h e i) -> p h e i", e=2, i=HD),
                        ones[:, 0:HD].unsqueeze(1).unsqueeze(1).broadcast_to([P, H // 2, 2, HD]), ALU.mult).then_inc(sem["c_vp_done"], 1)
                if s[0] in "ce" and s[2] == "p":
                    k, g = s[0], int(s[3])
                    pool.wait_ge(sem[f"{k}_rz"], now.group_done(k, g))
                    nc.gpsimd.tensor_tensor(sc[k][:, g % 2], sc[k][:, g % 2],
                                            rz[k][:, GH * g:GH * g + GH].unsqueeze(2).broadcast_to([P, GH, P]),
                                            ALU.mult).then_inc(sem[f"{k}_probs"], 1)
                if s == "a_qk":
                    pool.wait_ge(sem["a_qk.free"], now.done("a"))
                    pool.wait_ge(sem["a_tr2.full"], now.last("a"))
                    nc.gpsimd.tensor_tensor(a_qk[:, :], a_c[:, :], a_s[:, :], ALU.add).then_inc(sem["a_rotated"], 1)
                if s in ("c_kb0", "c_kb1"):
                    key_blocks(now, "c", "c", int(s[4]))
                if s == "d_xb":
                    pool.wait_ge(sem["c_o.free"], now.done("d"))
                    pool.wait_ge(sem["e_o.free"], now.last("d"))
                    nc.gpsimd.tensor_tensor(e_xb[:, :], now.slot("d", d_x)[:, :], gbo[:, :], ALU.add).then_inc(sem["e_xb_done"], 1)
                if s in ("d_kb0", "d_kb1"):
                    key_blocks(now, "e", "d", int(s[4]))

            run(pool, ORDERS["pool"], step)

        @block.scalar
        def _(act):
            act.wait_ge(sem["loaded"], 32)
            nc.scalar.activation(tg[:, :], c["g"], ACT.Tanh).then_inc(sem["setup_g"], 1)

            def begin(t):
                if t == LAG["b"]:
                    act.wait_ge(sem["loaded_b"], 16)
                    nc.scalar.activation(we_h[:, :], c["we"], ACT.Copy).then_inc(sem["setup_we_hi"], 1)
                if t == LAG["d"]:
                    act.wait_ge(sem["loaded_d"], 16)

            def copy(dst, src):
                return nc.scalar.activation(dst, src, ACT.Copy)

            def weigh(now, s):
                act.wait_ge(sem[f"{s}_two_done"], now.done(s))
                nc.scalar.activation(top[s]["e"][:, :], top[s]["mx"][:, 1:2], ACT.Exp, bias=top[s]["n"][:, 0:1]).then_inc(sem[f"{s}_e_done"], 1)

            def exps(now, s, g):
                act.wait_ge(sem[f"{s}_max"], now.group_done(s, g))
                act.wait_ge(sem[f"{s}_t.full"], now.group_done(s, g - 2))
                act.wait_ge(sem[f"{s}_rz"], now.group_last(s, g))
                for j in range(GH):
                    at = GH * g + j
                    ins = nc.scalar.activation(sc[s][:, g % 2, j], psum(f"{s}_s{g}")[:, j * P:(j + 1) * P], ACT.Exp,
                                               bias=mx[s][:, at:at + 1], accum_out=sums[s][:, at:at + 1])
                ins.then_inc(sem[f"{s}_s.free"], 1)

            def keep_probs(now, s, g):
                act.wait_ge(sem[f"{s}_t.full"], now.group_done(s, g))
                act.wait_ge(sem[f"{s}_av"], now.group_done(s, g - 2))
                ins = copy(pt[s][:, g % 2], psum(f"{s}_t{g}").rearrange("p (h q) -> p h q", h=GH))
                ins.then_inc(sem[f"{s}_t.free"], 1)

            def keys(now, step, s, bk, stage):
                act.wait_ge(sem[f"{step}.full"], now.done(stage))
                act.wait_ge(sem[f"{s}_kb_done"], now.half_last(stage, 1))
                for m in range(KT):
                    last = nc.scalar.activation(kt[s][:, m], psum(step)[:, (KT + m) * P:(KT + m + 1) * P], ACT.Identity,
                                                bias=bk[:, m:m + 1])
                last.then_inc(sem[f"{s}_kt_done"], 1)

            def queries(now, step, s, bq, stage):
                act.wait_ge(sem[f"{s}_kt_done"], now.done(stage))
                act.wait_ge(sem[f"{s}_s.full"], now.group_last(stage, 3))
                for m in range(KT):
                    last = nc.scalar.activation(qt[s][:, m], psum(step)[:, m * P:(m + 1) * P], ACT.Identity,
                                                bias=bq[:, m:m + 1], scale=SCALE)
                last.then_inc(sem[f"{step}.free"], 1)

            def step(now, s):
                if s == "a_tr":
                    act.wait_ge(sem["a_tr.full"], now.done("a"))
                    act.wait_ge(sem["c_qk.full"], now.slot_free("a"))
                    copy(now.slot("a", a_t)[:, :, :], psum(s).rearrange("p (m q) -> p m q", m=2 * KT)).then_inc(sem["a_tr.free"], 1)
                if s == "a_v":
                    act.wait_ge(sem["a_v.full"], now.done("a"))
                    act.wait_ge(sem["a_o.full"], now.last("a"))
                    copy(a_v[:, :], psum(s)[:, 0:D]).then_inc(sem["a_v.free"], 1)
                if s == "a_tr2":
                    act.wait_ge(sem["a_tr2.full"], now.done("a"))
                    act.wait_ge(sem["a_r.full"], now.last("a"))
                    copy(a_qkt[:, :, :], psum(s).rearrange("p (m q) -> p m q", m=2 * KT)).then_inc(sem["a_tr2.free"], 1)
                if s == "b_tr":
                    act.wait_ge(sem["b_tr.full"], now.done("b"))
                    act.wait_ge(sem["b_g.full"], now.last("b"))
                    act.wait_ge(sem["b_lo_done"], now.last("b"))
                    copy(b_t[:, :, :], psum(s)[:, 0:D].rearrange("p (m q) -> p m q", m=KT)).then_inc(sem["b_tr.free"], 1)
                if s == "b_hi":
                    act.wait_ge(sem["b_tr.free"], now.done("b"))
                    act.wait_ge(sem["b_m3.full"], now.last("b"))
                    copy(b_th[:, :, :], b_t[:, :, :]).then_inc(sem["b_hi_done"], 1)
                if s == "b_g":
                    weigh(now, "b")
                if s == "b_w":
                    act.wait_ge(sem["b_w.full"], now.done("b"))
                    act.wait_ge(sem["b_be.full"], now.last("b"))
                    copy(b_wtt[:, :], psum(s)[:, 0:P]).then_inc(sem["b_w.free"], 1)
                if s == "c_tr":
                    act.wait_ge(sem["c_tr.full"], now.done("c"))
                    act.wait_ge(sem["c_qk.full"], now.last("c"))
                    copy(c_t[:, :, :], psum(s)[:, 0:D].rearrange("p (m q) -> p m q", m=KT)).then_inc(sem["c_tr.free"], 1)
                if s == "c_k":
                    keys(now, "c_qk", "c", c["bk1"], "c")
                if s == "c_q":
                    queries(now, "c_qk", "c", bq1s, "c")
                if s[0] in "ce" and s[2] == "s":
                    exps(now, s[0], int(s[3]))
                if s[0] in "ce" and s[2] == "t" and s[3].isdigit():
                    keep_probs(now, s[0], int(s[3]))
                if s == "c_yt":
                    act.wait_ge(sem["c_av"], now.group_done("c", 3))
                    act.wait_ge(sem["c_o.full"], now.last("c"))
                    copy(yt["c"][:, :, :], psum("c_v0")[:, 0:D].rearrange("p (m q) -> p m q", m=KT)).then_inc(sem["c_yt.free"], 1)
                if s == "e_yt":
                    act.wait_ge(sem["e_av"], now.group_done("e", 3))
                    act.wait_ge(sem["e_o.full"], now.last("e"))
                    act.wait_ge(sem["e_bv_done"], now.done("e"))
                    for m in range(KT):
                        last = nc.scalar.activation(yt["e"][:, m], psum("e_v0")[:, m * P:(m + 1) * P], ACT.Identity,
                                                    bias=e_bv[:, m:m + 1])
                    last.then_inc(sem["e_yt.free"], 1)
                if s == "d_tr":
                    act.wait_ge(sem["d_tr.full"], now.done("d"))
                    act.wait_ge(sem["d_v.full"], now.last("d"))
                    act.wait_ge(sem["d_h.full"], now.last("d"))
                    for m in range(KT):
                        last = nc.scalar.activation(d_t[:, m], psum(s)[:, m * P:(m + 1) * P], ACT.Copy,
                                                    accum_out=d_pool[:, m:m + 1])
                    last.then_inc(sem["d_tr.free"], 1)
                if s == "d_lg":
                    weigh(now, "d")
                if s in ("d_c0", "d_c1", "d_c2"):
                    j = int(s[3])
                    act.wait_ge(sem["d_weights_done"], now.done("d"))
                    act.wait_ge(sem["d_v.full" if j == 2 else "d_qk.full"], now.last("d"))
                    nc.scalar.activation(d_wx[:, j], wx[:, 0, j * KT * D:(j + 1) * KT * D], ACT.Copy,
                                         scale=top["d"]["w"][:, 0:1]).then_inc(sem[f"d_c{j}_first"], 1)
                if s == "d_k":
                    act.wait_ge(sem["d_bx"], now.group_done("d", 3))
                    keys(now, "d_qk", "e", d_bx[:, KT:2 * KT], "d")
                if s == "d_q":
                    queries(now, "d_qk", "e", d_bx, "d")
                if s == "d_v":
                    act.wait_ge(sem["d_v.full"], now.done("d"))
                    act.wait_ge(sem["e_av"], now.group_last("d", 3))
                    copy(pairs_of_heads("e"), psum(s)[:, 0:D].rearrange("p (h e i) -> p h e i", e=2, i=HD)).then_inc(sem["d_v.free"], 1)

            run(act, ORDERS["act"], step, begin)

        @block.vector
        def _(dve):
            dve.wait_ge(sem["setup_g"], 1)
            dve.wait_ge(sem["loaded"], 32)
            nc.vector.tensor_scalar(gbc[:, :], c["bc1"], tg[:, 2:3], None, ALU.mult)
            nc.vector.tensor_scalar(gbo[:, :], c["bo"], tg[:, 3:4], None, ALU.mult)
            nc.vector.tensor_scalar(bq1s[:, :], c["bq1"], SCALE, None, ALU.mult)
            nc.vector.memset(ones[:, :], 1.0)
            nc.vector.memset(b_wt[:, :], 0.0)
            for s in "ce":
                nc.vector.memset(vp[s][:, :, :], 0.0)
            for e in range(E1):
                ins = nc.vector.tensor_scalar(bx[:, e, 0:KT], bx[:, e, 0:KT], SCALE, None, ALU.mult)
            ins.then_inc(sem["setup_done"], 1)
            dve.wait_ge(sem["setup_done"], 1)

            def begin(t):
                if t == LAG["b"]:
                    dve.wait_ge(sem["setup_we_hi"], 1)
                    nc.vector.tensor_tensor(we_l[:, :], c["we"], we_h[:, :].bitcast(F32), ALU.subtract).then_inc(sem["setup_we_lo"], 1)
                if t == LAG["d"]:
                    dve.wait_ge(sem["loaded_d"], 16)

            def carry_waits(n):
                nc.vector.memset(carrier[:, n:n + 1], 0.0)

            def residual(s, dst, base, gate):
                return nc.vector.scalar_tensor_tensor(dst[:, :], psum(s)[:, 0:D], tg[:, gate:gate + 1], base[:, :], ALU.mult, ALU.add)

            def layer_norm(now, s, part):
                x_in, xn_of = {"a": (a_x, a_xn), "b": (b_x, b_xn), "c": (c_x, c_xn), "d": (d_x, d_xn)}[s]
                turn = NORM_WITH[s]
                x_of = now.slot(turn, x_in)
                if part == "st":
                    if s == "a":
                        dve.wait_ge(now.slot("a", loaded), now.arrived("a", 32))
                    else:
                        dve.wait_ge(sem[{"b": "a_o.free", "c": "c_x_done", "d": "c_o.free"}[s]], now.done(turn))
                    dve.wait_ge(sem[f"{s}_mv_done"], now.last(turn))
                    nc.vector.bn_stats(stats[s][:, :], x_of[:, :]).then_inc(sem[f"{s}_stats_done"], 1)
                if part == "ag":
                    dve.wait_ge(sem[f"{s}_stats_done"], now.done(turn))
                    dve.wait_ge(sem[f"{s}_vareps_done"], now.last(turn))
                    dve.wait_ge(sem[f"{s}_xn_done"], now.last(turn))
                    carry_waits("abcd".index(s))
                    nc.vector.bn_aggr(mv[s][:, :], stats[s][:, :]).then_inc(sem[f"{s}_mv_done"], 1)
                if part == "nm":
                    dve.wait_ge(sem[f"{s}_rstd_done"], now.done(turn))
                    dve.wait_ge(sem[f"{s}_tr.full"], now.last(turn))
                    nc.vector.tensor_scalar(xn_of[:, :], x_of[:, :], mv[s][:, 0:1], rstd[s][:, 1:2], ALU.subtract,
                                            ALU.mult).then_inc(sem[f"{s}_xn_done"], 1)

            def top_two(now, s, part, logits, bias):
                it = top[s]
                if part == "g0":
                    dve.wait_ge(sem[f"{logits}.full"], now.done(s))
                    dve.wait_ge(sem[f"{s}_ix_done"], now.last(s))
                    nc.vector.tensor_tensor(it["lg"][:, :], psum(logits)[:, 0:8], bias, ALU.add).then_inc(sem[f"{logits}.free"], 1)
                if part == "g1":
                    dve.wait_ge(sem[f"{logits}.free"], now.done(s))
                    dve.wait_ge(sem[f"{s}_e_done"], now.last(s))
                    carry_waits(4 + "bd".index(s))
                    nc.vector.max(it["mx"][:, :], it["lg"][:, :]).then_inc(sem[f"{s}_max_done"], 1)
                if part == "g2":
                    dve.wait_ge(sem[f"{s}_max_done"], now.done(s))
                    dve.wait_ge(sem[f"{s}_if_done"], now.last(s))
                    nc.vector.tensor_scalar(it["n"][:, :], it["mx"][:, 0:1], -1.0, None, ALU.mult).then_inc(sem[f"{s}_two_done"], 1)
                    nc.vector.max_index(it["ix"][:, :], it["mx"][:, :], it["lg"][:, :]).then_inc(sem[f"{s}_ix_done"], 1)
                if part == "g3":
                    dve.wait_ge(sem[f"{s}_ix_done"], now.done(s))
                    dve.wait_ge(sem[f"{s}_placed"], now.last(s))
                    nc.vector.tensor_copy(it["if"][:, :], it["ix"][:, 0:2]).then_inc(sem[f"{s}_if_done"], 1)

            def weights_of(now, s, part, dst):
                it = top[s]
                if part == "w0":
                    dve.wait_ge(sem[f"{s}_e_done"], now.done(s))
                    nc.vector.tensor_scalar(it["s"][:, :], it["e"][:, :], 1.0, None, ALU.add).then_inc(sem[f"{s}_sum_done"], 1)
                if part == "w1":
                    dve.wait_ge(sem[f"{s}_sum_done"], now.done(s))
                    nc.vector.reciprocal(it["r"][:, 0:1], it["s"][:, :]).then_inc(sem[f"{s}_first_done"], 1)
                if part == "w2":
                    dve.wait_ge(sem[f"{s}_first_done"], now.done(s))
                    nc.vector.tensor_tensor(it["r"][:, 1:2], it["r"][:, 0:1], it["e"][:, :], ALU.mult).then_inc(sem[f"{s}_second_done"], 1)
                if part == "w3":
                    dve.wait_ge(sem[f"{s}_second_done"], now.done(s))
                    dve.wait_ge(sem[f"{s}_if_done"], now.done(s))
                    nc.vector.tensor_scalar(it["w1"][:, :], c["iota"], it["if"][:, 0:1], it["r"][:, 0:1], ALU.is_equal, ALU.mult)
                    nc.vector.tensor_scalar(it["w2"][:, :], c["iota"], it["if"][:, 1:2], it["r"][:, 1:2], ALU.is_equal,
                                            ALU.mult).then_inc(sem[f"{s}_placed"], 1)
                if part == "w4":
                    dve.wait_ge(sem[f"{s}_placed"], now.done(s))
                    nc.vector.tensor_tensor(dst, it["w1"][:, :], it["w2"][:, :], ALU.add).then_inc(sem[f"{s}_weights_done"], 1)

            def attention(now, s, part, g):
                at = slice(GH * g, GH * g + GH)
                if part == "m":
                    dve.wait_ge(sem[f"{s}_s.full"], now.group_done(s, g))
                    dve.wait_ge(sem[f"{s}_s.free"], now.group_last(s, g))
                    src = psum(f"{s}_s{g}").rearrange("p (h k) -> p h k", h=GH)
                    nc.vector.tensor_reduce(mx[s][:, at], src, axis=AX.X, op=ALU.max, negate=True).then_inc(sem[f"{s}_max"], 1)
                else:
                    dve.wait_ge(sem[f"{s}_s.free"], now.group_done(s, g))
                    dve.wait_ge(sem[f"{s}_probs"], now.group_last(s, g))
                    nc.vector.reciprocal(rz[s][:, at], sums[s][:, at]).then_inc(sem[f"{s}_rz"], 1)

            def step(now, s):
                if s[2:] in ("st", "ag", "nm"):
                    layer_norm(now, s[0], s[2:])
                if s in ("a_q0", "a_q1", "a_q2"):
                    pairs, turned, sin = (v.rearrange("p (i two) -> p i two", two=2) for v in (psum("a_qk"), a_s[:, :], c["sin"]))
                    if s == "a_q0":
                        dve.wait_ge(sem["a_qk.full"], now.done("a"))
                        dve.wait_ge(sem["a_rotated"], now.last("a"))
                        nc.vector.tensor_tensor(a_c[:, :], psum("a_qk"), c["cos"], ALU.mult)
                    elif s == "a_q1":
                        nc.vector.tensor_tensor(turned[:, :, 0], pairs[:, :, 1], sin[:, :, 0], ALU.mult)
                    else:
                        nc.vector.tensor_tensor(turned[:, :, 1], pairs[:, :, 0], sin[:, :, 1], ALU.mult).then_inc(sem["a_qk.free"], 1)
                if s == "a_r":
                    dve.wait_ge(sem["a_r.full"], now.done("a"))
                    dve.wait_ge(sem["a_o.full"], now.last("a"))
                    nc.vector.tensor_tensor(a_ret[:, :], psum(s)[:, 0:P], c["decay"], ALU.mult).then_inc(sem["a_r.free"], 1)
                if s == "a_o":
                    dve.wait_ge(sem["a_o.full"], now.done("a"))
                    dve.wait_ge(sem["c_x_done"], now.slot_free("a"))
                    residual(s, now.slot("a", b_x), now.slot("a", a_x), 0).then_inc(sem["a_o.free"], 1)
                if s in ("b_g0", "b_g1", "b_g2", "b_g3"):
                    top_two(now, "b", s[2:], "b_g", c["bgate"])
                if s in ("b_w0", "b_w1", "b_w2", "b_w3", "b_w4"):
                    if s == "b_w4":
                        dve.wait_ge(sem["b_w.full"], now.last("b"))
                        dve.wait_ge(sem["b_m3.free"], now.last("b"))
                    weights_of(now, "b", s[2:], b_wt[:, 0:8])
                if s == "b_be":
                    dve.wait_ge(sem["b_be.full"], now.done("b"))
                    dve.wait_ge(sem["c_x_done"], now.last("b"))
                    nc.vector.tensor_copy(b_acc[:, :], psum(s)[:, 0:D]).then_inc(sem["b_be.free"], 1)
                if s[:3] == "b_m":
                    j, i = int(s[3]), "ab".index(s[4])
                    e = 2 * j + i
                    if i:
                        dve.wait_ge(sem["b_half"], now.group_done("b", j))
                    else:
                        dve.wait_ge(sem[f"b_m{j}.full"], now.done("b"))
                        dve.wait_ge(sem[f"b_m{j - 1}.free" if j else "b_be.free"], now.done("b"))
                    nc.vector.scalar_tensor_tensor(b_acc[:, :], psum(s[:4])[:, i * D:(i + 1) * D], b_wt[:, e:e + 1], b_acc[:, :],
                                                   ALU.mult, ALU.add).then_inc(sem[f"b_m{j}.free" if i else "b_half"], 1)
                if s == "b_fin":
                    dve.wait_ge(sem["b_m3.free"], now.done("b"))
                    dve.wait_ge(sem["c_xb_done"], now.slot_free("b"))
                    dve.wait_ge(sem["c_xn_done"], now.slot_free("b"))
                    nc.vector.scalar_tensor_tensor(now.slot("b", c_x)[:, :], b_acc[:, :], tg[:, 1:2], now.slot("b", b_x)[:, :], ALU.mult,
                                                   ALU.add).then_inc(sem["c_x_done"], 1)
                if s[0] in "ce" and s[2] in "mr" and s[3:].isdigit():
                    attention(now, s[0], s[2], int(s[3]))
                if s == "c_o":
                    dve.wait_ge(sem["c_o.full"], now.done("c"))
                    dve.wait_ge(sem["c_xb_done"], now.done("c"))
                    dve.wait_ge(sem["e_xb_done"], now.slot_free("c"))
                    dve.wait_ge(sem["d_xn_done"], now.slot_free("c"))
                    residual(s, now.slot("c", d_x), c_xb, 2).then_inc(sem["c_o.free"], 1)
                if s == "e_o":
                    dve.wait_ge(sem["e_o.full"], now.done("e"))
                    dve.wait_ge(sem["e_xb_done"], now.done("e"))
                    dve.wait_ge(sem["stored"], now.count(16, -16 * LAG["e"]))
                    residual(s, e_out, e_xb, 3).then_inc(sem["e_o.free"], 1)
                if s == "d_h":
                    dve.wait_ge(sem["d_h.full"], now.done("d"))
                    dve.wait_ge(sem["d_hb_done"], now.last("d"))
                    nc.vector.tensor_scalar(d_h[:, :], psum(s)[:, 0:1], 1.0 / P, c["bh"], ALU.mult, ALU.add).then_inc(sem["d_h.free"], 1)
                if s == "d_hb":
                    dve.wait_ge(sem["d_h.free"], now.done("d"))
                    dve.wait_ge(sem["d_lg.full"], now.last("d"))
                    nc.vector.tensor_scalar(d_hb[:, :], ones[:, :], d_h[:, 0:1], 0.0, ALU.mult, ALU.max).then_inc(sem["d_hb_done"], 1)
                if s in ("d_g0", "d_g1", "d_g2", "d_g3"):
                    top_two(now, "d", s[2:], "d_lg", c["bl"])
                if s in ("d_w0", "d_w1", "d_w2", "d_w3", "d_w4"):
                    if s == "d_w4":
                        dve.wait_ge(sem["d_c2_first"], now.last("d"))
                        dve.wait_ge(sem["d_c2_done"], now.last("d"))
                        dve.wait_ge(sem["d_bx"], now.group_last("d", 3))
                    weights_of(now, "d", s[2:], top["d"]["w"][:, :])
                if s in ("d_b0", "d_b1", "d_b2", "d_b3"):
                    e, w = int(s[3]), top["d"]["w"]
                    if e == 0:
                        dve.wait_ge(sem["d_weights_done"], now.done("d"))
                        dve.wait_ge(sem["d_qk.free"], now.last("d"))
                        dve.wait_ge(sem["e_bv_done"], now.last("d"))
                        nc.vector.tensor_scalar(d_bx[:, :], bx[:, 0], w[:, 0:1], None, ALU.mult).then_inc(sem["d_bx"], 1)
                    else:
                        dve.wait_ge(sem["d_bx"], now.group_done("d", e - 1))
                        nc.vector.scalar_tensor_tensor(d_bx[:, :], bx[:, e], w[:, e:e + 1], d_bx[:, :], ALU.mult,
                                                       ALU.add).then_inc(sem["d_bx"], 1)
                if s[:3] == "d_c":
                    j, e = int(s[3]), 1 + "abc".index(s[4])
                    w, n = top["d"]["w"], KT * D
                    if e == 1:
                        dve.wait_ge(sem[f"d_c{j}_first"], now.done("d"))
                    else:
                        dve.wait_ge(sem[f"d_c{j}_{e - 1}"], now.done("d"))
                    nc.vector.scalar_tensor_tensor(d_wx[:, j], wx[:, e, j * n:(j + 1) * n], w[:, e:e + 1], d_wx[:, j],
                                                   ALU.mult, ALU.add).then_inc(sem[f"d_c{j}_done" if e == E1 - 1 else f"d_c{j}_{e}"], 1)
                if s == "d_bv":
                    dve.wait_ge(sem["d_bx"], now.group_done("d", 3))
                    dve.wait_ge(sem["e_yt.free"], now.last("d"))
                    nc.vector.tensor_copy(e_bv[:, :], d_bx[:, 2 * KT:3 * KT]).then_inc(sem["e_bv_done"], 1)

            run(dve, ORDERS["dve"], step, begin)

        @block.tensor
        def _(pe):
            pe.wait_ge(sem["loaded"], 32)
            pe.wait_ge(sem["setup_done"], 1)

            def begin(t):
                if t == LAG["b"]:
                    pe.wait_ge(sem["loaded_b"], 16)
                    pe.wait_ge(sem["setup_we_lo"], 1)
                if t == LAG["c"]:
                    pe.wait_ge(sem["loaded_c"], 16)
                if t == LAG["d"]:
                    pe.wait_ge(sem["loaded_d"], 16)

            def mm(dst, lhs, rhs, k=0, last=0):
                return nc.tensor.matmul(dst, lhs, rhs, start=k == 0, stop=k == last)

            def transposes(s, tiles):
                out = psum(s).rearrange("p (m q) -> p m q", m=2 * KT)
                for m, tile in enumerate(tiles):
                    ins = nc.tensor.transpose(out[:, m], tile, ident)
                return ins

            def halves(tile):
                return [tile[:, m * P:(m + 1) * P] for m in range(KT)]

            def by_tokens(s, lhs, rhs, n, at=0):
                for k in range(KT):
                    ins = mm(psum(s)[:, at:at + n], lhs[:, k], rhs[:, k], k, KT - 1)
                return ins

            def by_channels(s, at, w, rhs):
                for m in range(KT):
                    for k in range(KT):
                        ins = mm(psum(s)[:, (at + m) * P:(at + m + 1) * P], w[:, k, m * P:(m + 1) * P], rhs[:, k], k, KT - 1)
                return ins

            def attention(now, s, step):
                g = int(step[3])
                if step[2] == "s":
                    m, at = g * GH // E0, g * GH % E0
                    if g == 0:
                        pe.wait_ge(sem["d_qk.free" if s == "e" else "c_qk.free"], now.done(s))
                    if at == 0:
                        pe.wait_ge(sem[f"{s}_kb_done"], now.half_done(s, m))
                    mm(psum(step).rearrange("p (h k) -> p h k", h=GH), qt[s][:, m], kb[s][:, m, at:at + GH]).then_inc(sem[f"{s}_s.full"], 1)
                elif step[2] == "t":
                    pe.wait_ge(sem[f"{s}_probs"], now.group_done(s, g))
                    transposes(step, [sc[s][:, g % 2, j] for j in range(GH)]).then_inc(sem[f"{s}_t.full"], 1)
                else:
                    pe.wait_ge(sem[f"{s}_t.free"], now.group_done(s, g))
                    if g == 0:
                        pe.wait_ge(sem[f"{s}_vp_done" if s == "c" else "d_v.free"], now.done(s))
                    for j in range(GH):
                        pair, odd = (GH * g + j) // 2, j % 2
                        m, row = pair * 2 * HD // P, pair * 2 * HD % P
                        ins = nc.tensor.matmul(psum(step)[row:row + 2 * HD, m * P:(m + 1) * P],
                                               vp[s][:, pair, HD * odd:HD * odd + 2 * HD], pt[s][:, g % 2, j],
                                               start=odd == 0, stop=odd == 1, tile_position=(0, row))
                    ins.then_inc(sem[f"{s}_av"], 1)

            def step(now, s):
                if TAKES[s]:
                    pe.wait_ge(sem[now.reader(s)], now.released(s))
                heads = s in GROUPED
                full = sem[f"{s}.full"] if TAKES[s] and not heads else None
                if s == "a_tr":
                    pe.wait_ge(sem["a_xn_done"], now.done("a"))
                    transposes(s, halves(a_xn) + halves(now.slot("a", ctx))).then_inc(full, 1)
                if s == "a_qk":
                    pe.wait_ge(sem["a_tr.free"], now.done("a"))
                    a_of = now.slot("a", a_t)
                    by_tokens(s, a_of[:, 0:KT], wq0, D)
                    by_tokens(s, a_of[:, KT:2 * KT], wk0, D, at=D).then_inc(full, 1)
                if s == "a_v":
                    by_tokens(s, now.slot("a", a_t)[:, KT:2 * KT], wv0, D).then_inc(full, 1)
                if s == "a_tr2":
                    pe.wait_ge(sem["a_rotated"], now.done("a"))
                    transposes(s, halves(a_qk[:, 0:D]) + halves(a_qk[:, D:2 * D])).then_inc(full, 1)
                if s == "a_r":
                    pe.wait_ge(sem["a_tr2.free"], now.done("a"))
                    for k in range(KT):
                        ins = mm(psum(s)[:, 0:P], a_qkt[:, KT + k], a_qkt[:, k], k, KT - 1)
                    ins.then_inc(full, 1)
                if s == "a_o":
                    pe.wait_ge(sem["a_r.free"], now.done("a"))
                    pe.wait_ge(sem["a_v.free"], now.done("a"))
                    mm(psum(s)[:, 0:D], a_ret[:, :], a_v[:, :]).then_inc(full, 1)
                if s == "b_tr":
                    pe.wait_ge(sem["b_xn_done"], now.done("b"))
                    transposes(s, halves(b_xn)).then_inc(full, 1)
                if s == "b_g":
                    pe.wait_ge(sem["b_tr.free"], now.done("b"))
                    by_tokens(s, b_t, wgate, E0).then_inc(full, 1)
                if s == "b_w":
                    pe.wait_ge(sem["b_weights_done"], now.done("b"))
                    nc.tensor.transpose(psum(s)[:, 0:P], b_wt[:, :], ident).then_inc(full, 1)
                if s == "b_be":
                    pe.wait_ge(sem["b_w.free"], now.done("b"))
                    mm(psum(s)[:, 0:D], b_wtt[:, :], c["be"]).then_inc(full, 1)
                if s in ("b_m0", "b_m1", "b_m2", "b_m3"):
                    j = int(s[3])
                    experts = slice(2 * j * D, 2 * (j + 1) * D)
                    if j == 0:
                        pe.wait_ge(sem["b_lo_done"], now.done("b"))
                    passes = [(x, w, k) for x, w in ((b_th, we_hi), (b_tl, we_hi), (b_th, we_lo)) for k in range(KT)]
                    for n, (x, w, k) in enumerate(passes):
                        ins = mm(psum(s), x[:, k], w[:, k, experts], n, len(passes) - 1)
                    ins.then_inc(full, 1)
                if s == "c_tr":
                    pe.wait_ge(sem["c_xn_done"], now.done("c"))
                    transposes(s, halves(c_xn)).then_inc(full, 1)
                if s == "c_qk":
                    pe.wait_ge(sem["c_tr.free"], now.done("c"))
                    by_channels(s, 0, wq1, c_t)
                    by_channels(s, KT, wk1, now.slot("c", a_t)[:, KT:2 * KT]).then_inc(full, 1)
                if s == "d_tr":
                    pe.wait_ge(sem["d_xn_done"], now.done("d"))
                    transposes(s, halves(d_xn)).then_inc(full, 1)
                if s == "d_h":
                    pe.wait_ge(sem["d_tr.free"], now.done("d"))
                    for k in range(KT):
                        ins = mm(psum(s)[:, 0:1], wh[:, k], d_pool[:, k:k + 1], k, KT - 1)
                    ins.then_inc(full, 1)
                if s == "d_lg":
                    pe.wait_ge(sem["d_hb_done"], now.done("d"))
                    mm(psum(s)[:, 0:8], d_hb[:, :], c["wl"]).then_inc(full, 1)
                if s == "d_qk":
                    pe.wait_ge(sem["d_c0_done"], now.done("d"))
                    by_channels(s, 0, d_wx[:, 0].rearrange("p (k n) -> p k n", k=KT), d_t)
                    pe.wait_ge(sem["d_c1_done"], now.done("d"))
                    by_channels(s, KT, d_wx[:, 1].rearrange("p (k n) -> p k n", k=KT), d_t).then_inc(full, 1)
                if s == "d_v":
                    pe.wait_ge(sem["d_c2_done"], now.done("d"))
                    by_tokens(s, d_t, d_wx[:, 2].rearrange("p (k n) -> p k n", k=KT), D).then_inc(full, 1)
                if heads:
                    attention(now, s[0], s)
                if s in ("c_o", "e_o"):
                    pe.wait_ge(sem[f"{s[0]}_yt.free"], now.done(s[0]))
                    by_tokens(s, yt[s[0]], wc1 if s[0] == "c" else wo, D).then_inc(full, 1)

            run(pe, ORDERS["pe"], step, begin)


def shape_tables():
    f = np.float32
    base = (np.arange(0, D, 2, dtype=f) + f(0.4 * D)) / f(1.4 * D)
    pos = np.arange(P, dtype=f)
    scale = base[None, :] ** (pos[:, None] / f(512.0))
    freqs = f(1.0) / f(10000.0) ** (np.arange(D // 2, dtype=f) / f(D // 2))
    angle = pos[:, None] * freqs[None, :]
    sign = np.tile(np.array([-1.0, 1.0], f), D // 2)

    def twice(a):
        return np.repeat(a, 2, axis=1).astype(f)

    u, v = np.arange(P)[None, :], np.arange(P)[:, None]
    decay = np.where(u >= v, f(GAMMA) ** np.maximum(u - v, 0).astype(f), f(0))
    heads = (np.arange(P)[:, None] // HD == np.arange(E0)[None, :])
    rows = {
        "cos": np.concatenate([twice(np.cos(angle) * s) for s in (scale, f(1) / scale)], axis=1),
        "sin": np.concatenate([twice(np.sin(angle) * s) * sign for s in (scale, f(1) / scale)], axis=1),
        "decay": decay, "ident": np.eye(P), "heads": heads, "iota": np.tile(np.arange(E0), (P, 1)),
        "eps": np.tile(np.array([EPS, -0.5]), (P, 1)),
    }
    return np.concatenate([rows[name].astype(f).reshape(P, n) for name, n in TABLES], axis=1)


def laid_out(i):
    def tiles(w):
        return w.reshape(KT, P, -1).transpose(1, 0, 2).reshape(P, -1)

    def everywhere(v):
        v = v.reshape(1, -1)
        return np.broadcast_to(v, (P, v.shape[1]))

    def columns(v):
        return v.reshape(KT, P).T

    def wider(w, rows, cols, fill=0.0):
        out = np.full((rows, cols), fill, np.float32)
        out[:w.shape[0], :w.shape[1]] = w
        return out

    mixed = np.stack([i["L1_ffn_Wq"], i["L1_ffn_Wk"], i["L1_ffn_Wv"]], axis=1).reshape(E1, 3, KT, P, D)
    mixed_b = np.stack([i["L1_ffn_bq"], i["L1_ffn_bk"], i["L1_ffn_bv"]], axis=1).reshape(E1, 3, KT, P)
    gates = np.stack([i["g_xattn"][0], i["g_ffn"][0], i["g_xattn"][1], i["g_ffn"][1]])
    parts = {
        "wq0": tiles(i["L0_xattn_Wq"].T),
        "wk0": tiles(i["L0_xattn_Wk"].T), "wv0": tiles(i["L0_xattn_Wv"].T),
        "we": tiles(i["L0_ffn_We"].transpose(2, 0, 1).reshape(D, E0 * D)),
        "be": wider(i["L0_ffn_be"], P, D), "wgate": tiles(i["L0_ffn_Wg"]), "bgate": everywhere(i["L0_ffn_bg"]),
        "wq1": tiles(i["L1_xattn_Wq"].T), "wk1": tiles(i["L1_xattn_Wk"].T), "bq1": columns(i["L1_xattn_bq"]),
        "bk1": columns(i["L1_xattn_bk"]), "wc1": tiles(i["L1_xattn_Wc"].T), "bc1": everywhere(i["L1_xattn_bc"]),
        "wx": mixed.transpose(3, 0, 1, 2, 4).reshape(P, -1), "bx": mixed_b.transpose(3, 0, 1, 2).reshape(P, -1),
        "wh": tiles(i["L1_ffn_Wg1"]), "bh": i["L1_ffn_bg1"].reshape(P, 1), "wl": wider(i["L1_ffn_Wg2"], P, E0),
        "bl": everywhere(wider(i["L1_ffn_bg2"].reshape(1, E1), 1, E0, NEG)), "wo": tiles(i["L1_ffn_Wo"]),
        "bo": everywhere(i["L1_ffn_bo"]), "g": everywhere(gates),
    }
    return np.ascontiguousarray(np.concatenate([parts[name].reshape(P, n) for name, n in PACKED], axis=1))


def kernel(**inputs):
    import concourse.bacc as bacc
    from concourse.bass_utils import run_bass_kernel_spmd

    i = {name: np.asarray(a) for name, a in inputs.items()}
    arrays = {"x": np.ascontiguousarray(i["x"]), "ctx": np.ascontiguousarray(i["ctx_1024"]), "weights": laid_out(i),
              "tables": shape_tables()}
    nc = bacc.Bacc("TRN2", target_bir_lowering=False, num_devices=1)
    aps = [nc.dram_tensor(name, a.shape, F32, kind="ExternalInput").ap() for name, a in arrays.items()]
    out = nc.dram_tensor("out", (NB, P, D), F32, kind="ExternalOutput").ap()
    build(nc, *aps, out)
    result = run_bass_kernel_spmd(nc, [arrays], core_ids=[0])
    return result.results[0]["out"]
```
